# Optimizing a Trainium2 kernel written in Bass

```python
import numpy as np
import jax
import jax.numpy as jnp

def _softmax(x, axis=-1):
    return jax.nn.softmax(x, axis=axis)

def _gelu(x):
    return jax.nn.gelu(x, approximate=True)

def _silu(x):
    return jax.nn.silu(x)

def _sigmoid(x):
    return jax.nn.sigmoid(x)

def _layernorm(x, axis=-1, eps=1e-05):
    m = jnp.mean(x, axis=axis, keepdims=True)
    v = jnp.var(x, axis=axis, keepdims=True)
    return (x - m) / jnp.sqrt(v + eps)

def _scatter_add(tgt, idx, src, axis=0):
    return tgt.at[idx].add(src)

def _segment_sum(src, seg, n):
    return jax.ops.segment_sum(src, seg, n)
kernel_name = 'mk_prb_d2_jaxref_r8_b763f2'

def setup_inputs(seed: int=0):
    np.random.seed(seed)
    _w = jnp.asarray

    def _L0_attn_setup():
        import jax, jax.numpy as jnp
        import numpy as np
        HEADS = 16
        DIM_HEAD = 64
        T_MAX = DIM_HEAD

        def _cope(q, sim, pos_emb):
            G = jax.nn.sigmoid(sim)
            P = jnp.flip(jnp.cumsum(jnp.flip(G, axis=-1), axis=-1), axis=-1)
            P = jnp.minimum(P, T_MAX - 1)
            P_floor = jnp.floor(P)
            P_ceil_i = jnp.ceil(P).astype(jnp.int32)
            P_floor_i = P_floor.astype(jnp.int32)
            E = jnp.einsum('bnc,ct->bnt', q, pos_emb)
            E_ceil = jnp.take_along_axis(E, P_ceil_i, axis=-1)
            E_floor = jnp.take_along_axis(E, P_floor_i, axis=-1)
            w = P - P_floor
            return w * E_ceil + (1.0 - w) * E_floor
        key = jax.random.key(seed)
        ks = jax.random.split(key, 6)
        B, N, D = (1, 256, 128)
        inner = HEADS * DIM_HEAD
        return {'x': jax.random.normal(ks[0], (B, N, D), dtype=jnp.float32), 'Wq': jax.random.normal(ks[1], (D, inner), dtype=jnp.float32) * 0.02, 'Wkv': jax.random.normal(ks[2], (D, 2 * inner), dtype=jnp.float32) * 0.02, 'Wout': jax.random.normal(ks[3], (inner, D), dtype=jnp.float32) * 0.02, 'b_out': jnp.zeros((D,), dtype=jnp.float32), 'pos_emb': jax.random.normal(ks[4], (DIM_HEAD, T_MAX), dtype=jnp.float32) * 0.02}
    _L0_attn_in = _L0_attn_setup()

    def _L0_ffn_setup():
        import jax, jax.numpy as jnp
        import numpy as np
        E = 8
        K = 2
        D = 128
        H = 342
        B, S = (2, 256)

        def _moe_forward(x, centroid, Wg, bg, W1, b1, W2, b2):
            T = x.shape[0] * x.shape[1]
            xs = x.reshape(T, D)
            d2 = jnp.sum(xs * xs, axis=-1, keepdims=True) + jnp.sum(centroid * centroid, axis=-1)[None, :] - 2.0 * (xs @ centroid.T)
            dist = jnp.sqrt(jnp.maximum(d2, 1e-12))
            w, sel = jax.lax.top_k(dist, K)
            w = jax.nn.softmax(w.astype(jnp.float32), axis=1).astype(x.dtype)
            we = jnp.zeros((T, E), dtype=x.dtype).at[jnp.arange(T)[:, None], sel].add(w)
            out = jnp.zeros_like(xs)
            for e in range(E):
                h = jax.nn.silu(xs @ Wg[e] + bg[e]) * (xs @ W1[e] + b1[e])
                out = out + we[:, e:e + 1] * (h @ W2[e] + b2[e])
            return out.reshape(x.shape)
        key = jax.random.key(seed)
        ks = jax.random.split(key, 9)
        scale = 0.02
        return {'x': jax.random.normal(ks[0], (B, S, D), dtype=jnp.float32), 'centroid': jax.random.normal(ks[1], (E, D), dtype=jnp.float32), 'Wg': jax.random.normal(ks[2], (E, D, H), dtype=jnp.float32) * scale, 'bg': jnp.zeros((E, H), dtype=jnp.float32), 'W1': jax.random.normal(ks[3], (E, D, H), dtype=jnp.float32) * scale, 'b1': jnp.zeros((E, H), dtype=jnp.float32), 'W2': jax.random.normal(ks[4], (E, H, D), dtype=jnp.float32) * scale, 'b2': jnp.zeros((E, D), dtype=jnp.float32)}
    _L0_ffn_in = _L0_ffn_setup()

    def _L1_attn_setup():
        import jax, jax.numpy as jnp
        import numpy as np
        DIM = 128
        HEADS = 16
        DIM_HEAD = DIM // HEADS
        LATENT = DIM // 4
        SCALE = DIM_HEAD ** (-0.5)
        key = jax.random.key(seed)
        ks = jax.random.split(key, 8)
        B, S = (2, 256)
        init = lambda k, shape, fan_in: jax.random.normal(k, shape, jnp.float32) * fan_in ** (-0.5)
        return {'x': jax.random.normal(ks[0], (B, S, DIM), jnp.float32), 'Wq': init(ks[1], (DIM, DIM), DIM), 'bq': jnp.zeros((DIM,), jnp.float32), 'Wl': init(ks[2], (DIM, LATENT), DIM), 'bl': jnp.zeros((LATENT,), jnp.float32), 'Wk': init(ks[3], (LATENT, DIM), LATENT), 'bk': jnp.zeros((DIM,), jnp.float32), 'Wv': init(ks[4], (LATENT, DIM), LATENT), 'bv': jnp.zeros((DIM,), jnp.float32), 'Wo': init(ks[5], (DIM, DIM), DIM), 'bo': jnp.zeros((DIM,), jnp.float32)}
    _L1_attn_in = _L1_attn_setup()

    def _L1_ffn_setup():
        import jax, jax.numpy as jnp
        import numpy as np
        TOPK = 4
        key = jax.random.key(seed)
        ks = jax.random.split(key, 9)
        B, T, D = (4, 256, 128)
        E, H = (32, 128)
        HS = H * TOPK
        s = lambda k, shape, fan: jax.random.normal(k, shape, dtype=jnp.float32) / np.sqrt(fan)
        return {'x': jax.random.normal(ks[0], (B, T, D), dtype=jnp.float32), 'router_w': s(ks[1], (E, D), D), 'router_bias': jnp.zeros((E,), dtype=jnp.float32), 'gate_w': s(ks[2], (E, H, D), D), 'up_w': s(ks[3], (E, H, D), D), 'down_w': s(ks[4], (E, D, H), H), 'sgate_w': s(ks[5], (HS, D), D), 'sup_w': s(ks[6], (HS, D), D), 'sdown_w': s(ks[7], (D, HS), HS)}
    _L1_ffn_in = _L1_ffn_setup()
    _d = {'L0_attn_x': _L0_attn_in['x'], 'L0_attn_Wq': _L0_attn_in['Wq'], 'L0_attn_Wkv': _L0_attn_in['Wkv'], 'L0_attn_Wout': _L0_attn_in['Wout'], 'L0_attn_b_out': _L0_attn_in['b_out'], 'L0_attn_pos_emb': _L0_attn_in['pos_emb'], 'L0_ffn_centroid': _L0_ffn_in['centroid'], 'L0_ffn_Wg': _L0_ffn_in['Wg'], 'L0_ffn_bg': _L0_ffn_in['bg'], 'L0_ffn_W1': _L0_ffn_in['W1'], 'L0_ffn_b1': _L0_ffn_in['b1'], 'L0_ffn_W2': _L0_ffn_in['W2'], 'L0_ffn_b2': _L0_ffn_in['b2'], 'L1_attn_Wq': _L1_attn_in['Wq'], 'L1_attn_bq': _L1_attn_in['bq'], 'L1_attn_Wl': _L1_attn_in['Wl'], 'L1_attn_bl': _L1_attn_in['bl'], 'L1_attn_Wk': _L1_attn_in['Wk'], 'L1_attn_bk': _L1_attn_in['bk'], 'L1_attn_Wv': _L1_attn_in['Wv'], 'L1_attn_bv': _L1_attn_in['bv'], 'L1_attn_Wo': _L1_attn_in['Wo'], 'L1_attn_bo': _L1_attn_in['bo'], 'L1_ffn_router_w': _L1_ffn_in['router_w'], 'L1_ffn_router_bias': _L1_ffn_in['router_bias'], 'L1_ffn_gate_w': _L1_ffn_in['gate_w'], 'L1_ffn_up_w': _L1_ffn_in['up_w'], 'L1_ffn_down_w': _L1_ffn_in['down_w'], 'L1_ffn_sgate_w': _L1_ffn_in['sgate_w'], 'L1_ffn_sup_w': _L1_ffn_in['sup_w'], 'L1_ffn_sdown_w': _L1_ffn_in['sdown_w']}
    _x0 = _d['L0_attn_x']
    _d['L0_attn_x'] = jax.random.normal(jax.random.fold_in(jax.random.key(seed), 1), (8, 512, 128), dtype=_x0.dtype)
    del _x0
    return _d

def reference(L0_attn_x, L0_attn_Wq, L0_attn_Wkv, L0_attn_Wout, L0_attn_b_out, L0_attn_pos_emb, L0_ffn_centroid, L0_ffn_Wg, L0_ffn_bg, L0_ffn_W1, L0_ffn_b1, L0_ffn_W2, L0_ffn_b2, L1_attn_Wq, L1_attn_bq, L1_attn_Wl, L1_attn_bl, L1_attn_Wk, L1_attn_bk, L1_attn_Wv, L1_attn_bv, L1_attn_Wo, L1_attn_bo, L1_ffn_router_w, L1_ffn_router_bias, L1_ffn_gate_w, L1_ffn_up_w, L1_ffn_down_w, L1_ffn_sgate_w, L1_ffn_sup_w, L1_ffn_sdown_w):

    def _L0_attn_ref(x, Wq, Wkv, Wout, b_out, pos_emb):
        import jax, jax.numpy as jnp
        import numpy as np
        HEADS = 16
        DIM_HEAD = 64
        T_MAX = DIM_HEAD

        def _cope(q, sim, pos_emb):
            G = jax.nn.sigmoid(sim)
            P = jnp.flip(jnp.cumsum(jnp.flip(G, axis=-1), axis=-1), axis=-1)
            P = jnp.minimum(P, T_MAX - 1)
            P_floor = jnp.floor(P)
            P_ceil_i = jnp.ceil(P).astype(jnp.int32)
            P_floor_i = P_floor.astype(jnp.int32)
            E = jnp.einsum('bnc,ct->bnt', q, pos_emb)
            E_ceil = jnp.take_along_axis(E, P_ceil_i, axis=-1)
            E_floor = jnp.take_along_axis(E, P_floor_i, axis=-1)
            w = P - P_floor
            return w * E_ceil + (1.0 - w) * E_floor
        B, N, D = x.shape
        h, d = (HEADS, DIM_HEAD)
        scale = d ** (-0.5)
        q = x @ Wq
        kv = x @ Wkv
        k, v = jnp.split(kv, 2, axis=-1)

        def to_heads(t):
            return t.reshape(B, N, h, d).transpose(0, 2, 1, 3).reshape(B * h, N, d)
        q, k, v = (to_heads(q), to_heads(k), to_heads(v))
        sim = jnp.einsum('bid,bjd->bij', q, k) * scale
        sim = sim + _cope(q, sim, pos_emb)
        attn = jax.nn.softmax(sim, axis=-1)
        out = jnp.einsum('bij,bjd->bid', attn, v)
        out = out.reshape(B, h, N, d).transpose(0, 2, 1, 3).reshape(B, N, h * d)
        return out @ Wout + b_out

    def _L0_ffn_ref(x, centroid, Wg, bg, W1, b1, W2, b2):
        import jax, jax.numpy as jnp
        import numpy as np
        E = 8
        K = 2
        D = 128
        H = 342
        B, S = (2, 256)

        def _moe_forward(x, centroid, Wg, bg, W1, b1, W2, b2):
            T = x.shape[0] * x.shape[1]
            xs = x.reshape(T, D)
            d2 = jnp.sum(xs * xs, axis=-1, keepdims=True) + jnp.sum(centroid * centroid, axis=-1)[None, :] - 2.0 * (xs @ centroid.T)
            dist = jnp.sqrt(jnp.maximum(d2, 1e-12))
            w, sel = jax.lax.top_k(dist, K)
            w = jax.nn.softmax(w.astype(jnp.float32), axis=1).astype(x.dtype)
            we = jnp.zeros((T, E), dtype=x.dtype).at[jnp.arange(T)[:, None], sel].add(w)
            out = jnp.zeros_like(xs)
            for e in range(E):
                h = jax.nn.silu(xs @ Wg[e] + bg[e]) * (xs @ W1[e] + b1[e])
                out = out + we[:, e:e + 1] * (h @ W2[e] + b2[e])
            return out.reshape(x.shape)
        return _moe_forward(x, centroid, Wg, bg, W1, b1, W2, b2)

    def _L1_attn_ref(x, Wq, bq, Wl, bl, Wk, bk, Wv, bv, Wo, bo):
        import jax, jax.numpy as jnp
        import numpy as np
        DIM = 128
        HEADS = 16
        DIM_HEAD = DIM // HEADS
        LATENT = DIM // 4
        SCALE = DIM_HEAD ** (-0.5)
        B, S, D = x.shape
        H, Dh = (HEADS, DIM_HEAD)
        q = (x @ Wq + bq).reshape(B, S, H, Dh)
        latent = x @ Wl + bl
        k = (latent @ Wk + bk).reshape(B, S, H, Dh)
        v = (latent @ Wv + bv).reshape(B, S, H, Dh)
        scores = jnp.einsum('bihd,bjhd->bhij', q, k) * SCALE
        attn = jax.nn.softmax(scores, axis=-1)
        out = jnp.einsum('bhij,bjhd->bihd', attn, v).reshape(B, S, D)
        out = out @ Wo + bo
        return out

    def _L1_ffn_ref(x, router_w, router_bias, gate_w, up_w, down_w, sgate_w, sup_w, sdown_w):
        import jax, jax.numpy as jnp
        import numpy as np
        TOPK = 4
        B, T, D = x.shape
        flat = x.reshape(B * T, D)
        logits = flat.astype(jnp.float32) @ router_w.T + router_bias
        scores = jax.nn.softmax(logits, axis=-1)
        topk_scores, topk_idx = jax.lax.top_k(scores, TOPK)
        topk_scores = topk_scores / jnp.clip(topk_scores.sum(axis=-1, keepdims=True), 1e-12, None)
        h = jax.nn.silu(jnp.einsum('nd,ehd->neh', flat, gate_w)) * jnp.einsum('nd,ehd->neh', flat, up_w)
        expert_out = jnp.einsum('neh,edh->ned', h, down_w)
        sel = jnp.take_along_axis(expert_out, topk_idx[:, :, None], axis=1)
        out = (sel * topk_scores.astype(flat.dtype)[:, :, None]).sum(axis=1)
        out = out + jax.nn.silu(flat @ sgate_w.T) * (flat @ sup_w.T) @ sdown_w.T
        return out.reshape(B, T, D)
    x = L0_attn_x
    xn = _layernorm(x, axis=-1)
    x = x + _L0_attn_ref(xn, L0_attn_Wq, L0_attn_Wkv, L0_attn_Wout, L0_attn_b_out, L0_attn_pos_emb) + _L0_ffn_ref(xn, L0_ffn_centroid, L0_ffn_Wg, L0_ffn_bg, L0_ffn_W1, L0_ffn_b1, L0_ffn_W2, L0_ffn_b2)
    xn = _layernorm(x, axis=-1)
    x = x + _L1_attn_ref(xn, L1_attn_Wq, L1_attn_bq, L1_attn_Wl, L1_attn_bl, L1_attn_Wk, L1_attn_bk, L1_attn_Wv, L1_attn_bv, L1_attn_Wo, L1_attn_bo) + _L1_ffn_ref(xn, L1_ffn_router_w, L1_ffn_router_bias, L1_ffn_gate_w, L1_ffn_up_w, L1_ffn_down_w, L1_ffn_sgate_w, L1_ffn_sup_w, L1_ffn_sdown_w)
    return x

_drawn_inputs = setup_inputs


def setup_inputs(seed=0):
    import zlib

    import numpy as np

    out = dict(_drawn_inputs(seed))
    spreads = {'L0_attn_b_out': (0.0, 0.1),
     'L0_ffn_bg': (0.0, 0.61),
     'L0_ffn_b1': (0.0, 0.587),
     'L0_ffn_b2': (0.0, 0.1),
     'L1_attn_bq': (0.0, 0.534),
     'L1_attn_bl': (0.0, 0.1),
     'L1_attn_bk': (0.0, 0.8),
     'L1_attn_bv': (0.0, 0.1),
     'L1_attn_bo': (0.0, 0.1),
     'L1_ffn_router_bias': (0.0, 0.1)}
    factors = {'L0_attn_Wq': 8.0,
     'L0_attn_Wkv': 3.438,
     'L0_attn_Wout': 3.583,
     'L0_attn_pos_emb': 8.0,
     'L0_ffn_Wg': 3.199,
     'L0_ffn_W1': 3.196,
     'L0_ffn_W2': 3.011}
    for name, (base, spread) in spreads.items():
        noise = np.random.default_rng([zlib.crc32(name.encode()), seed]).standard_normal(out[name].shape)
        drawn = base * np.exp(spread * noise) if base else spread * noise
        out[name] = jnp.asarray(drawn.astype(out[name].dtype))
    for name, factor in factors.items():
        out[name] = (out[name] * factor).astype(out[name].dtype)
    return out
```

```python
from contextlib import ExitStack

import concourse.bass as bass
from concourse import mybir

F32 = mybir.dt.float32
BF16 = mybir.dt.bfloat16
I16 = mybir.dt.int16
U32 = mybir.dt.uint32
ALU = mybir.AluOpType
ACT = mybir.ActivationFunctionType
AX = mybir.AxisListType

P = 128


class Dims:

    def __init__(self, x, Wq, pos_emb, Wg, centroid, router_w, gate_all):
        self.B, self.S, self.D = x.shape
        self.T = self.B * self.S
        self.NT = self.T // P
        self.TB = self.S // P
        self.DH, self.TMAX = pos_emb.shape
        self.HEADS = Wq.shape[1] // self.DH
        self.PAIRS = self.HEADS // 2
        self.E0, _, self.H0 = Wg.shape
        self.HC = -(-self.H0 // P)
        self.HL = self.H0 - P * (self.HC - 1)
        self.E1 = router_w.shape[1]
        self.EA = gate_all.shape[0]
        self.HEADS1 = 16
        self.DH1 = self.D // self.HEADS1
        assert self.D == P and self.S == 512 and self.DH == 64 and self.TMAX == 64


class Core:

    def __init__(self, nc, ctx, d):
        def sb(name, shape, dt=F32):
            return ctx.enter_context(nc.sbuf_tensor(name, shape, dt))

        self.x = sb("x_tokens", [P, d.NT, P])
        self.xnT = sb("xn_T", [P, d.T])
        self.attn = sb("attn_out", [P, d.NT, P])
        self.gate0 = sb("gate0", [P, d.NT, d.E0])
        self.gate1 = sb("gate1", [P, d.NT, d.EA])
        self.ident = sb("ident", [P, P])
        self.ones_row = sb("ones_row", [1, P])
        self.ones_col = sb("ones_col", [P, 1])


def start_at_one(nc, semaphores, loads):
    with nc.Block() as block:

        @block.sync
        def _(sp):
            for s in semaphores:
                if all(s is not x for x in loads):
                    sp.sem_inc(s, 1)


def setup_phase(nc, core, d, x_in):
    with ExitStack() as ctx:
        x_loaded = ctx.enter_context(nc.semaphore("x_loaded"))
        filled = ctx.enter_context(nc.semaphore("const_filled"))
        block = ctx.enter_context(nc.Block())

        @block.sync
        def _(sp):
            view = x_in.rearrange("(t p) c -> p t c", p=P)
            for q in range(4):
                k = d.NT // 4
                sp.dma_start(core.x[:, q * k:(q + 1) * k, :], view[:, q * k:(q + 1) * k, :]).then_inc(x_loaded, 16)
            sp.wait_ge(x_loaded, 64)

        @block.gpsimd
        def _(pool):
            pool.memset(core.ident[:], 0.0).then_inc(filled, 1)
            pool.memset(core.ones_row[:], 1.0).then_inc(filled, 1)
            pool.memset(core.ones_col[:], 1.0).then_inc(filled, 1)
            pool.memset(core.gate1[:, :, d.E1:d.EA], 1.0).then_inc(filled, 1)
            pool.wait_ge(filled, 4)
            pool.affine_select(out=core.ident[:], in_=core.ident[:], compare_op=ALU.not_equal, fill=1.0,
                               base=0, pattern=[[-1, P]], channel_multiplier=1).then_inc(filled, 1)
            pool.wait_ge(filled, 5)


def norm_phase(nc, core, d, tag, router, router_rhs_in, router_row_in):
    distances = tag == "0"
    NE = d.E0 if distances else d.E1
    TB, NT = d.TB, d.NT
    with ExitStack() as ctx:
        def sb(name, shape, dt=F32):
            return ctx.enter_context(nc.sbuf_tensor(name + tag, shape, dt))

        counted = []

        def sem(name):
            counted.append(ctx.enter_context(nc.semaphore(name + tag)))
            return counted[-1]

        stats = sb("bn_stats", [P, 2, TB, 6])
        mean_var = sb("mean_var", [P, 2, TB, 2])
        std = sb("std", [P, 2, TB])
        rstd = sb("rstd", [P, 2, TB])
        xn = sb("xn", [P, 2, TB, P])
        square = sb("square", [P, TB, P])
        sumsq = sb("sumsq", [P, 2, TB])
        xg = sb("xn_T_group", [P, 2, TB * P])
        rhs = sb("router_rhs", [P, NE])
        row = sb("router_row", [1, NE])
        scores = sb("scores", [P, NT, NE])
        eps = sb("eps", [P, 1])
        turned = ctx.enter_context(nc.psum_tensor("turned" + tag, [P, 2, TB, P], F32))
        score_ps = ctx.enter_context(nc.psum_tensor("score_ps" + tag, [P, 2, 512], F32))

        router_loaded = sem("router_loaded")
        router_ready = sem("router_ready")
        eps_ready, wait_carried = sem("eps_ready"), sem("wait_carried")
        stats_done, aggr_done, std_done, rstd_done = sem("stats"), sem("aggr"), sem("std_s"), sem("rstd_s")
        xn_done, sq_done, turned_done, xg_done = sem("xn_s"), sem("sq_s"), sem("turned_s"), sem("xg_s")
        xnT_done, score_done, score_out = sem("xnT_s"), sem("score_s"), sem("score_out")
        start_at_one(nc, counted, (router_loaded,))
        with nc.Block() as block:

            @block.sync
            def _(sp):
                sp.dma_start(rhs[:], router_rhs_in).then_inc(router_loaded, 16)
                if not distances:
                    sp.dma_start(row[:], router_row_in).then_inc(router_loaded, 16)

            @block.vector
            def _(dve):
                dve.memset(eps[:], 1e-5).then_inc(eps_ready, 1)
                if distances:
                    dve.wait_ge(router_loaded, 16)
                    dve.tensor_tensor(square[:, 0, 0:NE], rhs[:], rhs[:], ALU.mult).then_inc(router_ready, 1)
                    dve.wait_ge(router_ready, 2)
                    dve.tensor_scalar(rhs[:], rhs[:], -2.0, None, ALU.mult).then_inc(router_ready, 1)
                    dve.wait_ge(router_ready, 4)
                    dve.tensor_copy(row[:], score_ps[0:1, 0, 0:NE]).then_inc(router_ready, 1)
                with dve.Fori(0, d.B // 2) as gg:
                    for s in range(2):
                        g = gg * 2 + s
                        for t in range(TB):
                            dve.bn_stats(stats[:, s, t, :], core.x[:, bass.ds(g * TB + t, 1), :]).then_inc(stats_done, 1)
                        dve.wait_ge(stats_done, (g + 1) * TB + 1)
                        dve.sem_inc(wait_carried, 1)
                        for t in range(TB):
                            dve.bn_aggr(mean_var[:, s, t, :], stats[:, s, t, :]).then_inc(aggr_done, 1)
                        dve.wait_ge(std_done, g + 2)
                        dve.reciprocal(rstd[:, s, :], std[:, s, :]).then_inc(rstd_done, 1)
                        dve.wait_ge(rstd_done, g + 2)
                        dve.wait_ge(turned_done, g * TB + 1)
                        for t in range(TB):
                            dve.tensor_scalar(xn[:, s, t, :], core.x[:, bass.ds(g * TB + t, 1), :],
                                              mean_var[:, s, t, 0:1], rstd[:, s, t:t + 1],
                                              ALU.subtract, ALU.mult).then_inc(xn_done, 1)
                        dve.wait_ge(xg_done, g + 2)
                        dve.tensor_copy(core.xnT[:, bass.ds(g * TB * P, TB * P)], xg[:, s, :]).then_inc(xnT_done, 1)
                        dve.wait_ge(score_done, g + 2)
                        psv = score_ps[:, s, 0:TB * NE].rearrange("p (t e) -> p t e", t=TB)
                        if distances:
                            for t in range(TB):
                                dve.wait_ge(sq_done, (g + 1) * TB + 1)
                                op = dve.tensor_scalar(scores[:, bass.ds(g * TB + t, 1), :], psv[:, t, :],
                                                       sumsq[:, s, t:t + 1], 1e-12, ALU.add, ALU.max)
                        else:
                            op = dve.tensor_copy(scores[:, bass.ds(g * TB, TB), :], psv)
                        op.then_inc(score_out, 1)

            @block.scalar
            def _(act):
                act.wait_ge(eps_ready, 2)
                with act.Fori(0, d.B // 2) as gg:
                    for s in range(2):
                        g = gg * 2 + s
                        act.wait_ge(aggr_done, (g + 1) * TB + 1)
                        act.activation(std[:, s, :], mean_var[:, s, :, 1], ACT.Sqrt, bias=eps[:]).then_inc(std_done, 1)
                        if distances:
                            act.wait_ge(xn_done, (g + 1) * TB + 1)
                            act.wait_ge(sq_done, g * TB + 1)
                            for t in range(TB):
                                act.activation(square[:, t, :], xn[:, s, t, :], ACT.Square,
                                               accum_out=sumsq[:, s, t:t + 1]).then_inc(sq_done, 1)
                        act.wait_ge(turned_done, (g + 1) * TB + 1)
                        act.copy(xg[:, s, :], turned[:, s, :, :]).then_inc(xg_done, 1)

            @block.tensor
            def _(pe):
                if distances:
                    pe.wait_ge(router_ready, 3)
                    pe.matmul(score_ps[0:1, 0, 0:NE], core.ones_col[:], square[:, 0, 0:NE], start=True,
                              stop=True).then_inc(router_ready, 1)
                    pe.wait_ge(router_ready, 5)
                else:
                    pe.wait_ge(router_loaded, 32)
                with pe.Fori(0, d.B // 2) as gg:
                    for s in range(2):
                        g = gg * 2 + s
                        pe.wait_ge(xn_done, (g + 1) * TB + 1)
                        pe.wait_ge(xg_done, g + 1)
                        for t in range(TB):
                            pe.transpose(turned[:, s, t, :], xn[:, s, t, :], core.ident[:]).then_inc(turned_done, 1)
                        pe.wait_ge(xg_done, g + 2)
                        pe.wait_ge(score_out, g + 1)
                        for t in range(TB):
                            out = score_ps[:, s, t * NE:(t + 1) * NE]
                            pe.matmul(out, xg[:, s, t * P:(t + 1) * P], rhs[:], start=True, stop=False)
                            op = pe.matmul(out, core.ones_row[:], row[:], start=False, stop=True)
                        op.then_inc(score_done, 1)

        router(nc, core, d, scores)


def routing_phase(nc, core, d, tag, scores, gates, topk, distances):
    NT, NE = scores.shape[1], scores.shape[2]
    with ExitStack() as ctx:
        def sb(name, shape, dt=F32):
            return ctx.enter_context(nc.sbuf_tensor(name + tag, shape, dt))

        best = sb("best8", [P, NT, 8])
        where = sb("where8", [P, NT, 8], U32)
        where_f = sb("where8_f", [P, NT, 8])
        numbers = sb("expert_numbers", [P, NE])
        hit = sb("hit", [P, NT, NE])
        picked = sb("picked", [P, NT, NE])
        top = sb("row_max", [P, NT])
        total = sb("row_sum", [P, NT])
        inv = sb("row_inv", [P, NT])
        step = ctx.enter_context(nc.semaphore("route_step" + tag))
        activated = ctx.enter_context(nc.semaphore("route_act" + tag))
        numbered = ctx.enter_context(nc.semaphore("route_numbers" + tag))
        shift_done = ctx.enter_context(nc.semaphore("route_shift" + tag))

        def wide(a):
            return a.unsqueeze(2).to_broadcast([P, NT, NE])

        with nc.Block() as block:

            @block.gpsimd
            def _(pool):
                pool.iota(numbers[:], pattern=[[1, NE]], base=0, channel_multiplier=0,
                          allow_small_or_imprecise_dtypes=True).then_inc(numbered, 1)

            @block.scalar
            def _(act):
                if distances:
                    act.activation(scores[:], scores[:], ACT.Sqrt).then_inc(activated, 1)
                act.wait_ge(shift_done, 1)
                act.activation(picked[:], picked[:], ACT.Exp).then_inc(activated, 1)

            @block.vector
            def _(dve):
                n = [0]

                def done(op):
                    op.then_inc(step, 1)
                    n[0] += 1
                    dve.wait_ge(step, n[0])

                a = 0
                if distances:
                    a = 1
                    dve.wait_ge(activated, 1)
                done(dve.tensor_reduce(top[:], scores[:], AX.X, ALU.max))
                dve.tensor_tensor(picked[:], scores[:], wide(top[:]), ALU.subtract).then_inc(shift_done, 1)
                dve.wait_ge(activated, a + 1)
                if not distances:
                    done(dve.tensor_reduce(total[:], picked[:], AX.X, ALU.add))
                    done(dve.reciprocal(inv[:], total[:]))
                    done(dve.tensor_tensor(scores[:], picked[:], wide(inv[:]), ALU.mult))
                    done(dve.tensor_copy(picked[:], scores[:]))
                for t in range(NT):
                    op = dve.max(best[:, t, :], scores[:, t, :])
                done(op)
                for t in range(NT):
                    op = dve.max_index(where[:, t, :], best[:, t, :], scores[:, t, :])
                done(op)
                done(dve.tensor_copy(where_f[:], where[:]))
                dve.wait_ge(numbered, 1)
                num = numbers[:].unsqueeze(1).to_broadcast([P, NT, NE])
                for k in range(topk):
                    out = gates if k == 0 else hit[:]
                    done(dve.tensor_tensor(out, num, wide(where_f[:, :, k]), ALU.is_equal))
                    if k:
                        done(dve.tensor_tensor(gates, gates, hit[:], ALU.add))
                done(dve.tensor_tensor(picked[:], picked[:], gates, ALU.mult))
                done(dve.tensor_reduce(total[:], picked[:], AX.X, ALU.add))
                if not distances:
                    done(dve.tensor_scalar(total[:], total[:], 1e-12, None, ALU.max))
                done(dve.reciprocal(inv[:], total[:]))
                done(dve.tensor_tensor(gates, picked[:], wide(inv[:]), ALU.mult))


def moe_phase(nc, core, d, tag, Wg, W1, W2, bias_g, bias_1, bias_2, gates, hidden):
    NE = Wg.shape[0]
    HC, HL = len(hidden), hidden[-1]
    H = sum(hidden)
    biased = bias_g is not None
    ONE = 96
    K = [h for h in hidden[:-1]] + [ONE + 1 if biased else HL]
    G, TB = d.B, d.TB
    N = TB * P
    assert NE % 2 == 0 and (not biased or HL <= ONE)
    with ExitStack() as ctx:
        def sb(name, shape, dt=F32):
            return ctx.enter_context(nc.sbuf_tensor(name + tag, shape, dt))

        def sem(name):
            return ctx.enter_context(nc.semaphore(name + tag))

        wg = [sb(f"wg{s}_", [P, H]) for s in range(2)]
        w1 = [sb(f"w1{s}_", [P, H]) for s in range(2)]
        w2 = [sb(f"w2{s}_", [P, HC, P]) for s in range(2)]
        bg = [sb(f"bg{s}_", [P, HC]) for s in range(2)]
        b1 = [sb(f"b1{s}_", [P, HC]) for s in range(2)]
        silu = sb("silu", [P, 2, N])
        hT = sb("hT", [P, 2, HC, N])
        gate_ps = ctx.enter_context(nc.psum_tensor("gate_ps" + tag, [P, 2, N], F32))
        up_ps = ctx.enter_context(nc.psum_tensor("up_ps" + tag, [P, 2, N], F32))
        down_ps = ctx.enter_context(nc.psum_tensor("down_ps" + tag, [P, 2, TB, P], F32))
        w_loaded = [sem(f"w_loaded{s}_") for s in range(2)]
        w_free = [sem(f"w_free{s}_") for s in range(2)]
        gate_done, up_done, silu_done, h_done = sem("gate_s"), sem("up_s"), sem("silu_s"), sem("h_s")
        down_done, added = sem("down_s"), sem("added_s")
        ones_set = sem("ones_set")
        LOADS = 7 if biased else 3

        with nc.Block() as block:

            @block.sync
            def _(sp):
                if biased:
                    sp.wait_ge(ones_set, 4)
                with sp.Fori(0, NE // 2) as ee:
                    for s in range(2):
                        e = ee * 2 + s
                        sp.wait_ge(w_free[s], ee + 1)

                        def load(dst, src):
                            sp.dma_start(dst, src).then_inc(w_loaded[s], 16)

                        load(wg[s][:], Wg[bass.ds(e, 1)].rearrange("o k h -> k (o h)"))
                        load(w1[s][:], W1[bass.ds(e, 1)].rearrange("o k h -> k (o h)"))
                        if not biased:
                            load(w2[s][:, 0, :], W2[bass.ds(e, 1)].rearrange("o h c -> h (o c)"))
                        else:
                            F = (HC - 1) * P
                            w2e = W2[bass.ds(e, 1)].rearrange("o h c -> (o h) c")
                            load(w2[s][:, 0:HC - 1, :], w2e[0:F, :].rearrange("(k p) c -> p k c", p=P))
                            load(w2[s][0:HL, HC - 1, :], w2e[F:H, :])
                            load(w2[s][ONE:ONE + 1, HC - 1, :], bias_2[bass.ds(e, 1), :])
                            for dst, src in ((bg[s], bias_g), (b1[s], bias_1)):
                                load(dst[:], src[bass.ds(e, 1)].rearrange("o p k -> p (o k)"))

            @block.gpsimd
            def _(pool):
                for s in range(2):
                    pool.sem_inc(w_free[s], 1)
                if biased:
                    for s in range(2):
                        pool.memset(hT[:, s, HC - 1, :], 0.0).then_inc(ones_set, 1)
                        pool.memset(w2[s][:, HC - 1, :], 0.0).then_inc(ones_set, 1)
                    pool.wait_ge(ones_set, 4)
                    pool.memset(hT[ONE:ONE + 1, :, HC - 1, :], 1.0).then_inc(ones_set, 1)

            LW = 16 * LOADS

            def groups_lagged(eng, first, second, ee, s):
                def at(g, r):
                    return g, r, (ee * 2 + s) * G + g
                first(*at(0, 0))
                with eng.Fori(0, G // 2 - 1) as k:
                    first(*at(k * 2 + 1, 1))
                    second(*at(k * 2, 0))
                    first(*at(k * 2 + 2, 0))
                    second(*at(k * 2 + 1, 1))
                first(*at(G - 1, 1))
                second(*at(G - 2, 0))
                second(*at(G - 1, 1))

            @block.tensor
            def _(pe):
                if biased:
                    pe.wait_ge(ones_set, 5)
                with pe.Fori(0, NE // 2) as ee:
                    for s in range(2):
                        pe.wait_ge(w_loaded[s], (ee + 1) * LW)

                        def gate_up(g, r, n):
                            rhs = core.xnT[:, bass.ds(g * N, N)]
                            for c in range(HC):
                                slot = (r * HC + c) % 2
                                pe.wait_ge(h_done, n * HC + c + 1)
                                cols = slice(c * P, c * P + hidden[c])
                                pe.matmul(gate_ps[0:hidden[c], slot, :], wg[s][:, cols], rhs,
                                          start=True, stop=True).then_inc(gate_done, 1)
                                pe.matmul(up_ps[0:hidden[c], slot, :], w1[s][:, cols], rhs,
                                          start=True, stop=True).then_inc(up_done, 1)

                        def down(g, r, n):
                            pe.wait_ge(h_done, (n + 1) * HC + 2)
                            pe.wait_ge(added, n + 1)
                            for t in range(TB):
                                for c in range(HC):
                                    op = pe.matmul(down_ps[:, r, t, :], hT[0:K[c], r, c, t * P:(t + 1) * P],
                                                   w2[s][0:K[c], c, :], start=(c == 0), stop=(c == HC - 1))
                            op.then_inc(down_done, 1)

                        groups_lagged(pe, gate_up, down, ee, s)

            @block.scalar
            def _(act):
                with act.Fori(0, NE // 2) as ee:
                    for s in range(2):
                        if biased:
                            act.wait_ge(w_loaded[s], (ee + 1) * LW)
                        with act.Fori(0, G // 2) as gg:
                            for r in range(2):
                                n = (ee * 2 + s) * G + gg * 2 + r
                                for c in range(HC):
                                    slot = (r * HC + c) % 2
                                    rows = hidden[c]
                                    act.wait_ge(gate_done, n * HC + c + 1)
                                    act.wait_ge(h_done, n * HC + c + 1)
                                    if biased:
                                        op = act.activation(silu[0:rows, slot, :], gate_ps[0:rows, slot, :], ACT.Silu,
                                                            bias=bg[s][0:rows, c:c + 1])
                                    else:
                                        op = act.activation(silu[0:rows, slot, :], gate_ps[0:rows, slot, :], ACT.Silu)
                                    op.then_inc(silu_done, 1)

            @block.vector
            def _(dve):
                for free in (h_done, h_done, added, added):
                    dve.sem_inc(free, 1)
                with dve.Fori(0, NE // 2) as ee:
                    for s in range(2):
                        def hidden_product(g, r, n):
                            for c in range(HC):
                                slot = (r * HC + c) % 2
                                rows = hidden[c]
                                dve.wait_ge(silu_done, n * HC + c + 1)
                                dve.wait_ge(up_done, n * HC + c + 1)
                                h, u, z = hT[0:rows, r, c, :], up_ps[0:rows, slot, :], silu[0:rows, slot, :]
                                if biased:
                                    op = dve.scalar_tensor_tensor(out=h, in0=u, scalar=b1[s][0:rows, c:c + 1],
                                                                  in1=z, op0=ALU.add, op1=ALU.mult)
                                else:
                                    op = dve.tensor_tensor(h, u, z, ALU.mult)
                                op.then_inc(h_done, 1)

                        def add(g, r, n):
                            e = ee * 2 + s
                            dve.wait_ge(down_done, n + 1)
                            for t in range(TB):
                                xt = core.x[:, bass.ds(g * TB + t, 1), :].rearrange("p o c -> p (o c)")
                                we = gates[:, bass.ds(g * TB + t, 1), bass.ds(e, 1)].rearrange("p o c -> p (o c)")
                                op = dve.scalar_tensor_tensor(out=xt, in0=down_ps[:, r, t, :], scalar=we, in1=xt,
                                                              op0=ALU.mult, op1=ALU.add)
                            op.then_inc(added, 1)

                        groups_lagged(dve, hidden_product, add, ee, s)
                        dve.sem_inc(w_free[s], 1)


def cope_attention_phase(nc, core, d, tag, HOT, Wq, Wkv, Wout, pos_emb):
    S, TB, DH, TM = d.S, d.TB, d.DH, d.TMAX
    H1 = HOT + 1
    UNITS = d.B * d.HEADS
    BITS = (32, 16, 8, 4, 2, 1)
    NTAB = TM + 2
    scale = DH ** -0.5
    with ExitStack() as ctx:
        def sb(name, shape, dt=F32):
            return ctx.enter_context(nc.sbuf_tensor(name + tag, shape, dt))

        def ps(name, shape):
            return ctx.enter_context(nc.psum_tensor(name + tag, shape, F32))

        counted = []

        def sem(name):
            counted.append(ctx.enter_context(nc.semaphore(name + tag)))
            return counted[-1]

        wqkv = sb("wqkv", [P, 3, P])
        wout = sb("wout", [P, P])
        table_w = sb("table_w", [P, NTAB])
        pe_raw = sb("pe_raw", [P, TM])
        xb = sb("x_batch", [P, S])
        qT = sb("qT", [P, S])
        kT = sb("kT", [P, S])
        v = sb("v", [P, TB, P])
        logits = sb("logits", [P, 2, TB, S])
        g_sig = sb("g_sig", [P, 2, TB, H1])
        slope = sb("slope", [P, 2, TB, HOT])
        ends = sb("table_ends", [P, 2, TB, 2])
        pos = sb("pos", [P, TB, H1])
        n_raw = sb("n_raw", [P, TB, H1], I16)
        n_pos = sb("n_pos", [P, TB, H1], BF16)
        shift = sb("shift", [P, TB, H1], I16)
        masks = sb("masks", [P, 3, TB, HOT], I16)
        frac = sb("frac", [P, TB, HOT])
        stepped = sb("stepped", [P, TB, HOT], BF16)
        gain = sb("gain", [P, TB, H1])
        e_floor = sb("e_floor", [P, TB, H1])
        cope = sb("cope", [P, TB, HOT])
        row_max = sb("row_max", [P, TB])
        neg_max = sb("neg_max", [P, 2, TB])
        row_sum = sb("row_sum", [P, 2, TB])
        row_inv = sb("row_inv", [P, 2, TB])
        diag = sb("diag", [P, TB, P])
        probsT = sb("probsT", [P, 2, TB, P])
        outT = sb("outT", [P, S])
        y_sb = sb("y", [P, TB, P])
        cap = sb("cap", [P, TB, H1], BF16)
        keep = sb("keep", [P, TB, H1], BF16)
        one = sb("one", [P, TB, H1], BF16)
        key = sb("key", [P, TB, H1], I16)

        scores_ps = ps("scores_ps", [P, TB, S])
        small_ps = ps("small_ps", [P, S])
        turn_ps = ps("turn_ps", [P, 2, S])
        out_ps = ps("out_ps", [P, S])

        w_loaded, wout_loaded, pe_loaded = sem("w_loaded"), sem("wout_loaded"), sem("pe_loaded")
        const_done = sem("const_done")
        table_step = sem("table_step")
        xb_ready, q_done, k_done, v_done = sem("xb_ready"), sem("q_done"), sem("k_done"), sem("v_done")
        qT_ready, kT_ready, v_ready = sem("qT_ready"), sem("kT_ready"), sem("v_ready")
        y_kept, y_added = sem("y_kept"), sem("y_added")
        scores_done, table_done, logits_ready = sem("scores_done"), sem("table_done"), sem("logits_ready")
        tanh_done, g_ready, slope_ready = sem("tanh_done"), sem("g_ready"), sem("slope_ready")
        pos_ready, n_raw_ready, n_ready, shift_ready = sem("pos_r"), sem("n_raw_r"), sem("n_r"), sem("shift_r")
        mask_ready, slope_step = sem("mask_r"), sem("slope_step")
        frac_ready, stepped_ready, gain_ready = sem("frac_r"), sem("stepped_r"), sem("gain_r")
        floor_ready, rise_ready, cope_ready = sem("floor_r"), sem("rise_r"), sem("cope_r")
        logits_hot, max_ready, neg_ready = sem("logits_hot"), sem("max_r"), sem("neg_r")
        exp_done, inv_ready, diag_ready = sem("exp_done"), sem("inv_r"), sem("diag_r")
        turned, probs_ready, out_done, outT_ready = sem("turned_p"), sem("probs_r"), sem("out_done"), sem("outT_r")
        y_done = sem("y_done")
        wait_carried, pool_wait_carried = sem("wait_carried"), sem("pool_wait_carried")

        def flat(t):
            return t.rearrange("p b h -> p (b h)")

        start_at_one(nc, counted, (w_loaded, wout_loaded, pe_loaded))
        with nc.Block() as block:

            @block.sync
            def _(sp):
                sp.dma_start(pe_raw[0:DH, :], pos_emb).then_inc(pe_loaded, 16)
                sp.dma_start(pe_raw[DH:2 * DH, :], pos_emb).then_inc(pe_loaded, 16)
                with sp.Fori(0, d.B * d.PAIRS) as pair:
                    p = pair % d.PAIRS
                    sp.wait_ge(v_done, pair + 1)
                    for i, (w, off) in enumerate(((Wq, 0), (Wkv, 0), (Wkv, d.HEADS * DH))):
                        sp.dma_start(wqkv[:, i, :], w[:, bass.ds(off + p * P, P)]).then_inc(w_loaded, 16)
                    sp.wait_ge(y_done, pair + 1)
                    sp.dma_start(wout[:], Wout[bass.ds(p * P, P), :]).then_inc(wout_loaded, 16)

            @block.gpsimd
            def _(pool):
                pool.memset(core.attn[:], 0.0).then_inc(const_done, 1)
                pool.memset(flat(cap[:]), float(TM - 1)).then_inc(const_done, 1)
                pool.memset(flat(keep[:]), 1.0).then_inc(const_done, 1)
                pool.memset(flat(one[:]), 1.0).then_inc(const_done, 1)
                pool.iota(key[:], pattern=[[0, TB], [1, H1]], base=-1, channel_multiplier=0,
                          allow_small_or_imprecise_dtypes=True).then_inc(const_done, 1)
                pool.wait_ge(const_done, 6)
                pool.memset(cap[:, :, 0:1], 0.0).then_inc(const_done, 1)
                pool.memset(keep[:, :, 0:1], 0.0).then_inc(const_done, 1)
                for s in range(2):
                    pool.memset(g_sig[:, s, :, 0:1], 0.0).then_inc(const_done, 1)
                pool.memset(gain[:], 0.0).then_inc(const_done, 1)
                pool.wait_ge(const_done, 11)

                def passed(m, h):
                    pool.wait_ge(slope_step, (m + 1) * len(BITS) + 1)
                    pool.wait_ge(floor_ready, m + 1)
                    pool.sem_inc(pool_wait_carried, 1)
                    pool.tensor_copy(gain[:, :, 0:1], ends[:, h, :, 0:1]).then_inc(gain_ready, 1)
                    pool.wait_ge(stepped_ready, m + 2)
                    pool.tensor_tensor(gain[:, :, 2:H1], stepped[:, :, 1:HOT], slope[:, h, :, 0:HOT - 1],
                                       ALU.mult).then_inc(gain_ready, 1)

                def fraction(m):
                    pool.wait_ge(n_ready, m + 2)
                    pool.tensor_tensor(stepped[:], n_pos[:, :, 1:H1], n_pos[:, :, 0:HOT],
                                       ALU.subtract).then_inc(stepped_ready, 1)

                def rise(m, h):
                    pool.wait_ge(frac_ready, m + 2)
                    pool.wait_ge(logits_hot, m + 1)
                    pool.tensor_tensor(cope[:], frac[:], slope[:, h], ALU.mult).then_inc(rise_ready, 1)
                    pool.wait_ge(floor_ready, m + 2)
                    pool.wait_ge(rise_ready, m + 2)
                    pool.tensor_tensor(cope[:], cope[:], e_floor[:, :, 1:H1], ALU.add).then_inc(cope_ready, 1)

                def fraction_value(m):
                    pool.tensor_tensor(frac[:], pos[:, :, 1:H1], n_pos[:, :, 1:H1],
                                       ALU.subtract).then_inc(frac_ready, 1)

                def inverse(m, h):
                    pool.wait_ge(inv_ready, m + 2)
                    pool.wait_ge(turned, TB * m + 1)
                    pool.tensor_tensor(diag[:], core.ident[:].unsqueeze(1).to_broadcast([P, TB, P]),
                                       row_inv[:, h].unsqueeze(2).to_broadcast([P, TB, P]),
                                       ALU.mult).then_inc(diag_ready, 1)

                def add_output(pair):
                    pool.wait_ge(y_kept, pair + 2)
                    y = core.attn[:, bass.ds(pair // d.PAIRS * TB, TB), :]
                    pool.tensor_tensor(y, y_sb[:], y, ALU.add).then_inc(y_added, 1)

                def pool_pair(pair, first):
                    for h in range(2):
                        n = pair * 2 + h
                        if not (first and h == 0):
                            passed(n - 1, 1 - h)
                            rise(n - 1, 1 - h)
                        fraction(n)
                        fraction_value(n)
                        if not first:
                            inverse(n - 2, h)
                    if not first:
                        add_output(pair - 1)

                pool_pair(0, True)
                with pool.Fori(1, UNITS // 2) as pair:
                    pool_pair(pair, False)
                passed(UNITS - 1, 1)
                rise(UNITS - 1, 1)
                inverse(UNITS - 2, 0)
                inverse(UNITS - 1, 1)
                add_output(UNITS // 2 - 1)

            @block.vector
            def _(dve):
                dve.wait_ge(pe_loaded, 32)
                dve.memset(table_w[:], 0.0).then_inc(table_step, 1)
                dve.wait_ge(table_step, 2)
                dve.tensor_tensor(table_w[:, 0:TM - 1], pe_raw[:, 1:TM], pe_raw[:, 0:TM - 1],
                                  ALU.subtract).then_inc(table_step, 1)
                dve.tensor_copy(table_w[:, TM:TM + 1], pe_raw[:, 0:1]).then_inc(table_step, 1)
                dve.tensor_copy(table_w[:, TM + 1:TM + 2], pe_raw[:, TM - 1:TM]).then_inc(table_step, 1)
                dve.wait_ge(const_done, 11)

                def positions(n, h):
                    dve.wait_ge(g_ready, n + 2)
                    dve.wait_ge(frac_ready, n + 1)
                    dve.tensor_tensor_scan(flat(pos[:]), flat(g_sig[:, h]), flat(cap[:]), 0.0,
                                           ALU.add, ALU.min).then_inc(pos_ready, 1)
                    dve.wait_ge(pos_ready, n + 2)
                    dve.tensor_scalar(flat(n_raw[:]), flat(pos[:]), -0.5, None, ALU.add).then_inc(n_raw_ready, 1)
                    dve.wait_ge(n_raw_ready, n + 2)
                    dve.tensor_tensor_scan(flat(n_pos[:]), flat(one[:]), flat(n_raw[:]), -1.0,
                                           ALU.add, ALU.min).then_inc(n_ready, 1)
                    dve.wait_ge(n_ready, n + 2)
                    dve.tensor_tensor(flat(shift[:]), flat(key[:]), flat(n_pos[:]),
                                      ALU.subtract).then_inc(shift_ready, 1)

                def floors(m):
                    dve.wait_ge(gain_ready, 2 * (m + 1) + 1)
                    dve.wait_ge(cope_ready, m + 1)
                    dve.tensor_tensor_scan(flat(e_floor[:]), flat(keep[:]), flat(gain[:]), 0.0,
                                           ALU.mult, ALU.add).then_inc(floor_ready, 1)

                def look_up(n, h):
                    nb = len(BITS)

                    def mask(i):
                        dve.tensor_scalar(masks[:, i % 3], shift[:, :, 1:H1], BITS[i], None,
                                          ALU.bitwise_and).then_inc(mask_ready, 1)
                    dve.wait_ge(shift_ready, n + 2)
                    mask(0)
                    dve.wait_ge(slope_ready, n + 2)
                    for i, far in enumerate(BITS):
                        if i + 1 < nb:
                            mask(i + 1)
                        dve.wait_ge(mask_ready, n * nb + i + 2)
                        if i:
                            dve.wait_ge(slope_step, n * nb + i + 1)
                        dve.sem_inc(wait_carried, 1)
                        dve.copy_predicated(slope[:, h, :, far:HOT][:, :, ::-1], masks[:, i % 3, :, far:HOT][:, :, ::-1],
                                            slope[:, h, :, 0:HOT - far][:, :, ::-1]).then_inc(slope_step, 1)

                def maxima(m, h):
                    dve.wait_ge(cope_ready, m + 2)
                    dve.wait_ge(logits_ready, m + 2)
                    hot = logits[:, h, :, 0:HOT]
                    dve.tensor_tensor(hot, hot, cope[:], ALU.add).then_inc(logits_hot, 1)
                    dve.wait_ge(logits_hot, m + 2)
                    dve.tensor_reduce(row_max[:], logits[:, h], AX.X, ALU.max).then_inc(max_ready, 1)
                    dve.wait_ge(max_ready, m + 2)
                    dve.tensor_scalar(neg_max[:, h], row_max[:], -1.0, None, ALU.mult).then_inc(neg_ready, 1)

                def inverse_sum(m, h):
                    dve.wait_ge(exp_done, TB * (m + 1) + 1)
                    dve.reciprocal(row_inv[:, h], row_sum[:, h]).then_inc(inv_ready, 1)

                def dve_pair(pair, first):
                    for h in range(2):
                        n = pair * 2 + h
                        positions(n, h)
                        if not (first and h == 0):
                            floors(n - 1)
                        if not first:
                            inverse_sum(n - 2, h)
                        look_up(n, h)
                        if not (first and h == 0):
                            maxima(n - 1, 1 - h)

                dve_pair(0, True)
                with dve.Fori(1, UNITS // 2) as pair:
                    dve_pair(pair, False)
                floors(UNITS - 1)
                inverse_sum(UNITS - 2, 0)
                maxima(UNITS - 1, 1)
                inverse_sum(UNITS - 1, 1)

            @block.scalar
            def _(act):
                act.sem_inc(probs_ready, 1)

                def front(pair, h, first):
                    n = pair * 2 + h
                    act.wait_ge(scores_done, n + 2)
                    if not first:
                        act.wait_ge(pos_ready, n)
                    act.activation(g_sig[:, h, :, 1:H1], scores_ps[:, :, 0:HOT], ACT.Tanh,
                                   scale=0.5 * scale).then_inc(tanh_done, 1)
                    act.wait_ge(tanh_done, n + 2)
                    act.activation(g_sig[:, h, :, 1:H1], g_sig[:, h, :, 1:H1], ACT.Copy, bias=0.5,
                                   scale=0.5).then_inc(g_ready, 1)
                    act.wait_ge(table_done, n + 2)
                    if not first:
                        act.wait_ge(cope_ready, n)
                    tab = small_ps[:, 0:TB * NTAB].rearrange("p (b t) -> p b t", b=TB)
                    act.copy(ends[:, h], tab[:, :, TM:NTAB])
                    for k in range(0, HOT, TM):
                        w = min(TM, HOT - k)
                        op = act.copy(slope[:, h, :, k:k + w], tab[:, :, 0:w])
                    op.then_inc(slope_ready, 1)

                def keep_scores(pair, h):
                    op = act.activation(logits[:, h, :, 0:HOT], scores_ps[:, :, 0:HOT], ACT.Copy, scale=scale)
                    if HOT < S:
                        act.wait_ge(slope_ready, pair * 2 + h + 2)
                        for b in range(TB):
                            op = act.activation(logits[:, h, b, HOT:S], scores_ps[:, b, HOT:S], ACT.Identity,
                                                bias=ends[:, h, b, 1:2], scale=scale)
                    op.then_inc(logits_ready, 1)

                def back(m, h):
                    act.wait_ge(neg_ready, m + 2)
                    for b in range(TB):
                        act.activation(logits[:, h, b, :], logits[:, h, b, :], ACT.Exp, bias=neg_max[:, h, b:b + 1],
                                       accum_out=row_sum[:, h, b:b + 1]).then_inc(exp_done, 1)
                    for c in range(TB):
                        act.wait_ge(turned, TB * m + c + 2)
                        act.wait_ge(out_done, TB * m + c + 2)
                        act.copy(probsT[:, c % 2], turn_ps[:, c % 2, :].rearrange("p (b q) -> p b q", b=TB)
                                 ).then_inc(probs_ready, 1)
                    act.wait_ge(out_done, TB * (m + 1) + 3)
                    act.wait_ge(y_done, m // 2 + 1)
                    act.copy(outT[h * DH:(h + 1) * DH, :], out_ps[h * DH:(h + 1) * DH, :]).then_inc(outT_ready, 1)

                def keep_output(pair):
                    act.wait_ge(y_done, pair + 2)
                    act.wait_ge(y_added, pair + 1)
                    act.copy(y_sb[:], small_ps[:].rearrange("p (t c) -> p t c", t=TB)).then_inc(y_kept, 1)

                def act_pair(pair, first):
                    act.wait_ge(v_done, pair + 1)
                    act.copy(xb[:], core.xnT[:, bass.ds(pair // d.PAIRS * S, S)]).then_inc(xb_ready, 1)
                    act.wait_ge(q_done, pair + 2)
                    act.copy(qT[:], small_ps[:]).then_inc(qT_ready, 1)
                    act.wait_ge(k_done, pair + 2)
                    act.copy(kT[:], small_ps[:]).then_inc(kT_ready, 1)
                    front(pair, 0, first)
                    if not first:
                        back(pair * 2 - 2, 0)
                    keep_scores(pair, 0)
                    front(pair, 1, first)
                    if not first:
                        back(pair * 2 - 1, 1)
                        keep_output(pair - 1)
                    act.wait_ge(v_done, pair + 2)
                    act.copy(v[:], small_ps[:].rearrange("p (t c) -> p t c", t=TB)).then_inc(v_ready, 1)
                    keep_scores(pair, 1)

                act_pair(0, True)
                with act.Fori(1, UNITS // 2) as pair:
                    act_pair(pair, False)
                back(UNITS - 2, 0)
                back(UNITS - 1, 1)
                keep_output(UNITS // 2 - 1)

            @block.tensor
            def _(pe):
                pe.wait_ge(table_step, 5)
                pe.sem_inc(out_done, 1)
                pe.sem_inc(out_done, 1)


                def project_qk(pair):
                    pe.wait_ge(w_loaded, 48 * (pair + 1))
                    pe.wait_ge(xb_ready, pair + 2)
                    pe.wait_ge(v_ready, pair + 1)
                    pe.matmul(small_ps[:], wqkv[:, 0, :], xb[:], start=True, stop=True).then_inc(q_done, 1)
                    pe.wait_ge(qT_ready, pair + 2)
                    pe.matmul(small_ps[:], wqkv[:, 1, :], xb[:], start=True, stop=True).then_inc(k_done, 1)

                def scores(pair, h):
                    n = pair * 2 + h
                    rows = slice(h * DH, (h + 1) * DH)
                    pe.wait_ge(kT_ready, pair + 2)
                    pe.wait_ge(logits_ready, n + 1)
                    for b in range(TB):
                        op = pe.matmul(scores_ps[:, b, :], qT[rows, b * P:(b + 1) * P], kT[rows, :], start=True, stop=True)
                    op.then_inc(scores_done, 1)
                    if h == 1:
                        pe.wait_ge(slope_ready, n + 1)
                    for b in range(TB):
                        op = pe.matmul(small_ps[:, b * NTAB:(b + 1) * NTAB], qT[rows, b * P:(b + 1) * P], table_w[rows, :],
                                       start=True, stop=True)
                    op.then_inc(table_done, 1)

                def back(m, h):
                    rows = slice(h * DH, (h + 1) * DH)
                    pe.wait_ge(exp_done, TB * (m + 1) + 1)
                    pe.wait_ge(diag_ready, m + 2)

                    def turn(c):
                        pe.wait_ge(probs_ready, TB * m + c + 1)
                        for b in range(TB):
                            op = pe.matmul(turn_ps[:, c % 2, b * P:(b + 1) * P], logits[:, h, b, c * P:(c + 1) * P],
                                           diag[:, b, :], start=True, stop=True)
                        op.then_inc(turned, 1)

                    def weigh(c):
                        pe.wait_ge(probs_ready, TB * m + c + 3)
                        pe.matmul(out_ps[rows, :], v[:, c, rows], probsT[:, c % 2].rearrange("p b q -> p (b q)"),
                                  start=(c == 0), stop=(c == TB - 1)).then_inc(out_done, 1)

                    pe.wait_ge(outT_ready, m + 1)
                    turn(0)
                    for c in range(TB):
                        if c + 1 < TB:
                            turn(c + 1)
                        weigh(c)

                def output(pair):
                    pe.wait_ge(outT_ready, 2 * (pair + 1) + 1)
                    pe.wait_ge(wout_loaded, 16 * (pair + 1))
                    for t in range(TB):
                        op = pe.matmul(small_ps[:, t * P:(t + 1) * P], outT[:, t * P:(t + 1) * P], wout[:],
                                       start=True, stop=True)
                    op.then_inc(y_done, 1)

                def project_v(pair):
                    for t in range(TB):
                        op = pe.matmul(small_ps[:, t * P:(t + 1) * P], xb[:, t * P:(t + 1) * P], wqkv[:, 2, :],
                                       start=True, stop=True)
                    op.then_inc(v_done, 1)

                def pe_pair(pair, first):
                    project_qk(pair)
                    scores(pair, 0)
                    if not first:
                        back(pair * 2 - 2, 0)
                    scores(pair, 1)
                    if not first:
                        back(pair * 2 - 1, 1)
                    pe.wait_ge(slope_ready, pair * 2 + 3)
                    if not first:
                        output(pair - 1)
                        pe.wait_ge(y_kept, pair + 1)
                    project_v(pair)

                pe_pair(0, True)
                with pe.Fori(1, UNITS // 2) as pair:
                    pe_pair(pair, False)
                back(UNITS - 2, 0)
                back(UNITS - 1, 1)
                pe.wait_ge(v_ready, UNITS // 2 + 1)
                output(UNITS // 2 - 1)


def residual_phase(nc, core, d, b_out):
    with ExitStack() as ctx:
        b_row = ctx.enter_context(nc.sbuf_tensor("b_row", [1, P], F32))
        bias_ps = ctx.enter_context(nc.psum_tensor("bias_ps", [P, P], F32))
        loaded = ctx.enter_context(nc.semaphore("b_loaded"))
        spread = ctx.enter_context(nc.semaphore("b_spread"))
        summed = ctx.enter_context(nc.semaphore("residual_summed"))
        with nc.Block() as block:

            @block.sync
            def _(sp):
                sp.dma_start(b_row[:], b_out).then_inc(loaded, 16)

            @block.tensor
            def _(pe):
                pe.wait_ge(loaded, 16)
                pe.matmul(bias_ps[:], core.ones_row[:], b_row[:], start=True, stop=True).then_inc(spread, 1)

            @block.vector
            def _(dve):
                dve.tensor_tensor(core.x[:], core.x[:], core.attn[:], ALU.add).then_inc(summed, 1)
                dve.wait_ge(summed, 1)
                dve.wait_ge(spread, 1)
                dve.tensor_tensor(core.x[:], core.x[:], bias_ps[:].unsqueeze(1).to_broadcast([P, d.NT, P]),
                                  ALU.add).then_inc(summed, 1)


def latent_projection_phase(nc, core, d, qT, kT, v, Wq, Wl, Wk, Wv, biases):
    S, TB = d.S, d.TB
    L = Wl.shape[1]
    with ExitStack() as ctx:
        def sb(name, shape, dt=F32):
            return ctx.enter_context(nc.sbuf_tensor("lat_" + name, shape, dt))

        counted = []

        def sem(name):
            counted.append(ctx.enter_context(nc.semaphore("lat_" + name)))
            return counted[-1]

        wq, wl = sb("wq", [P, P]), sb("wl", [P, L])
        wk, wv = sb("wk", [L, P]), sb("wv", [L + 1, P])
        bias = sb("bias", [P, 3])
        latT = sb("latT", [L + 1, 2, S])
        q_ps, k_ps, l_ps, v_ps = [ctx.enter_context(nc.psum_tensor(f"lat_{n}_ps", [P, 2, S], F32)) for n in "qklv"]
        loaded, ones_set = sem("loaded"), sem("ones_set")
        q_done, l_done, k_done, v_done = sem("q_done"), sem("l_done"), sem("k_done"), sem("v_done")
        q_out, l_out, k_out, v_out = sem("q_out"), sem("l_out"), sem("k_out"), sem("v_out")
        start_at_one(nc, counted, (loaded,))
        with nc.Block() as block:

            @block.sync
            def _(sp):
                for dst, src in ((wq[:], Wq), (wl[:], Wl), (wk[:], Wk), (wv[0:L, :], Wv), (wv[L:L + 1, :], biases["v"]),
                                 (bias[:, 0:1], biases["q"]), (bias[:, 1:2], biases["k"]), (bias[0:L, 2:3], biases["l"])):
                    sp.dma_start(dst, src).then_inc(loaded, 16)

            @block.gpsimd
            def _(pool):
                pool.memset(latT[L:L + 1], 1.0).then_inc(ones_set, 1)

            @block.tensor
            def _(pe):
                pe.wait_ge(loaded, 8 * 16)
                pe.wait_ge(ones_set, 2)
                with pe.Fori(0, d.B // 2) as gg:
                    for s in range(2):
                        g = gg * 2 + s
                        x = core.xnT[:, bass.ds(g * S, S)]
                        pe.wait_ge(l_out, g + 1)
                        pe.matmul(l_ps[0:L, s, :], wl[:], x, start=True, stop=True).then_inc(l_done, 1)
                        pe.wait_ge(q_out, g + 1)
                        pe.matmul(q_ps[:, s, :], wq[:], x, start=True, stop=True).then_inc(q_done, 1)
                        pe.wait_ge(l_out, g + 2)
                        pe.wait_ge(k_out, g + 1)
                        pe.matmul(k_ps[:, s, :], wk[:], latT[0:L, s, :], start=True, stop=True).then_inc(k_done, 1)
                        pe.wait_ge(v_out, g + 1)
                        for t in range(TB):
                            op = pe.matmul(v_ps[:, s, t * P:(t + 1) * P], latT[:, s, t * P:(t + 1) * P], wv[:],
                                           start=True, stop=True)
                        op.then_inc(v_done, 1)

            @block.scalar
            def _(act):
                act.wait_ge(loaded, 8 * 16)
                with act.Fori(0, d.B // 2) as gg:
                    for s in range(2):
                        g = gg * 2 + s
                        act.wait_ge(l_done, g + 2)
                        act.wait_ge(v_done, g + 1)
                        act.activation(latT[0:L, s, :], l_ps[0:L, s, :], ACT.Identity, bias=bias[0:L, 2:3]).then_inc(l_out, 1)
                        act.wait_ge(q_done, g + 2)
                        act.activation(qT[:, bass.ds(g * S, S)], q_ps[:, s, :], ACT.Identity,
                                       bias=bias[:, 0:1]).then_inc(q_out, 1)

            @block.vector
            def _(dve):
                dve.wait_ge(loaded, 8 * 16)
                with dve.Fori(0, d.B // 2) as gg:
                    for s in range(2):
                        g = gg * 2 + s
                        dve.wait_ge(k_done, g + 2)
                        dve.tensor_scalar(kT[:, bass.ds(g * S, S)], k_ps[:, s, :], bias[:, 1:2], None,
                                          ALU.add).then_inc(k_out, 1)
                        dve.wait_ge(v_done, g + 2)
                        dve.tensor_copy(v[:, bass.ds(g * S, S)], v_ps[:, s, :]).then_inc(v_out, 1)


def latent_attention_phase(nc, core, d, qT, kT, v, aT):
    S, TB, DH, HG = d.S, d.TB, d.DH1, 4
    UNITS = d.B * d.HEADS1
    GROUPS = d.HEADS1 // HG
    with ExitStack() as ctx:
        def sb(name, shape, dt=F32):
            return ctx.enter_context(nc.sbuf_tensor("la_" + name, shape, dt))

        counted = []

        def sem(name):
            counted.append(ctx.enter_context(nc.semaphore("la_" + name)))
            return counted[-1]

        def ps(name, shape):
            return ctx.enter_context(nc.psum_tensor("la_" + name, shape, F32))

        own = sb("own", [P, d.HEADS1])
        own_v = sb("own_v", [P, d.HEADS1, P])
        qh = sb("qh", [P, 2, S])
        vh = sb("vh", [P, 2, TB, P])
        probs = sb("probs", [P, 2, TB, S])
        row_max, neg_max = sb("row_max", [P, 2, TB]), sb("neg_max", [P, 2, TB])
        row_sum, row_inv = sb("row_sum", [P, 2, TB]), sb("row_inv", [P, 2, TB])
        diag = sb("diag", [P, 2, TB, P])
        probsT = sb("probsT", [P, 2, S])
        scores_ps = ps("scores_ps", [P, TB, S])
        turn_ps = ps("turn_ps", [P, 2, S])
        out_ps = ps("out_ps", [P, 2, S])
        masks_set = sem("masks_set")
        qh_ready, vh_ready, scores_done = sem("qh_ready"), sem("vh_ready"), sem("scores_done")
        max_ready, neg_ready, exp_done = sem("max_ready"), sem("neg_ready"), sem("exp_done")
        inv_ready, diag_ready, turned = sem("inv_ready"), sem("diag_ready"), sem("turned")
        turned_a, turned_b = sem("probsT_a"), sem("probsT_b")
        weighed, group_added = sem("weighed"), sem("group_added")

        start_at_one(nc, counted, ())
        with nc.Block() as block:

            @block.gpsimd
            def _(pool):
                pool.memset(own[:], DH ** -0.5).then_inc(masks_set, 1)
                pool.memset(own_v[:], 1.0).then_inc(masks_set, 1)
                pool.memset(aT[:], 0.0).then_inc(masks_set, 1)
                pool.wait_ge(masks_set, 4)
                pool.affine_select(out=own[:], in_=own[:], compare_op=ALU.is_ge, fill=0.0, base=0,
                                   pattern=[[-DH, d.HEADS1]], channel_multiplier=1).then_inc(masks_set, 1)
                pool.affine_select(out=own_v[:], in_=own_v[:], compare_op=ALU.is_ge, fill=0.0, base=0,
                                   pattern=[[-DH, d.HEADS1], [1, P]], channel_multiplier=0).then_inc(masks_set, 1)
                pool.wait_ge(masks_set, 6)
                pool.affine_select(out=own[:], in_=own[:], compare_op=ALU.is_ge, fill=0.0, base=DH - 1,
                                   pattern=[[DH, d.HEADS1]], channel_multiplier=-1).then_inc(masks_set, 1)
                pool.affine_select(out=own_v[:], in_=own_v[:], compare_op=ALU.is_ge, fill=0.0, base=DH - 1,
                                   pattern=[[DH, d.HEADS1], [-1, P]], channel_multiplier=0).then_inc(masks_set, 1)
                pool.wait_ge(masks_set, 8)
                pool.sem_inc(masks_set, 1)

                def masked(n, u, it):
                    b, h = it // GROUPS, (it % GROUPS) * HG + u
                    s = u % 2
                    pool.wait_ge(scores_done, TB * n + 1)
                    pool.tensor_tensor(qh[:, s], qT[:, bass.ds(b * S, S)], own[:, bass.ds(h, 1)].to_broadcast([P, S]),
                                       ALU.mult).then_inc(qh_ready, 1)

                def masked_v(n, u, it):
                    b, h = it // GROUPS, (it % GROUPS) * HG + u
                    s = u % 2
                    pool.wait_ge(weighed, TB * n + 1)
                    pool.tensor_tensor(vh[:, s], v[:, bass.ds(b * S, S)].rearrange("p (t c) -> p t c", t=TB),
                                       own_v[:, bass.ds(h, 1), :].to_broadcast([P, TB, P]), ALU.mult).then_inc(vh_ready, 1)

                def spread(n, s):
                    pool.wait_ge(inv_ready, n + 2)
                    pool.tensor_tensor(diag[:, s], core.ident[:].unsqueeze(1).to_broadcast([P, TB, P]),
                                       row_inv[:, s].unsqueeze(2).to_broadcast([P, TB, P]), ALU.mult).then_inc(diag_ready, 1)

                with pool.Fori(0, d.B * GROUPS) as it:
                    for u in range(HG):
                        n = it * HG + u
                        masked(n, u, it)
                        masked_v(n, u, it) 
                        spread(n, u % 2)

            @block.tensor
            def _(pe):
                pe.wait_ge(masks_set, 9)

                def scores(n, u, it):
                    b = it // GROUPS
                    pe.wait_ge(qh_ready, n + 2)
                    for blk in range(TB):
                        pe.wait_ge(exp_done, TB * n - TB + blk + 1 + TB + 1)
                        pe.matmul(scores_ps[:, blk, :], qh[:, u % 2, blk * P:(blk + 1) * P], kT[:, bass.ds(b * S, S)],
                                  start=True, stop=True).then_inc(scores_done, 1)

                def back(n, u, it):
                    s = u % 2
                    pe.wait_ge(exp_done, TB * (n + 1) + TB + 1)
                    pe.wait_ge(diag_ready, n + 2)
                    pe.wait_ge(vh_ready, n + 2)

                    def turn(c):
                        half = (turned_a, turned_b)[c % 2]
                        pe.wait_ge(half, 2 * n + c // 2 + 1)
                        for blk in range(TB):
                            op = pe.matmul(turn_ps[:, c % 2, blk * P:(blk + 1) * P], probs[:, s, blk, c * P:(c + 1) * P],
                                           diag[:, s, blk, :], start=True, stop=True)
                        op.then_inc(turned, 1)

                    def weigh(c):
                        half = (turned_a, turned_b)[c % 2]
                        pe.wait_ge(half, 2 * n + c // 2 + 2)
                        pe.matmul(out_ps[:, 0, :], vh[:, s, c, :], probsT[:, c % 2],
                                  start=(u == 0 and c == 0), stop=(u == HG - 1 and c == TB - 1)).then_inc(weighed, 1)

                    turn(0)
                    for c in range(TB):
                        if c + 1 < TB:
                            turn(c + 1)
                        if c == 0 and u == 0:
                            pe.wait_ge(group_added, it + 1)
                        weigh(c)

                with pe.Fori(0, d.B * GROUPS) as it:
                    for u in range(HG):
                        n = it * HG + u
                        scores(n, u, it)
                        back(n, u, it)

            @block.scalar
            def _(act):
                for _ in range(TB):
                    act.sem_inc(exp_done, 1)
                with act.Fori(0, d.B * GROUPS) as it:
                    for u in range(HG):
                        n = it * HG + u
                        s = u % 2
                        for blk in range(TB):
                            if blk % 2 == 0:
                                act.wait_ge(neg_ready, 2 * n + blk // 2 + 2)
                            act.activation(probs[:, s, blk, :], scores_ps[:, blk, :], ACT.Exp, bias=neg_max[:, s, blk:blk + 1],
                                           accum_out=row_sum[:, s, blk:blk + 1]).then_inc(exp_done, 1)
                        for c in (0, 2):
                            act.wait_ge(turned, TB * n + c + 2)
                            act.wait_ge(weighed, TB * n + max(c - 1, 0) + 1)
                            act.copy(probsT[:, 0], turn_ps[:, 0, :]).then_inc(turned_a, 1)

            @block.vector
            def _(dve):
                with dve.Fori(0, d.B * GROUPS) as it:
                    for u in range(HG):
                        n = it * HG + u
                        s = u % 2
                        for half in range(2):
                            two = slice(2 * half, 2 * half + 2)
                            dve.wait_ge(scores_done, TB * n + 2 * half + 3)
                            dve.tensor_reduce(row_max[:, s, two], scores_ps[:, two, :], AX.X, ALU.max).then_inc(max_ready, 1)
                            dve.wait_ge(max_ready, 2 * n + half + 2)
                            dve.tensor_scalar(neg_max[:, s, two], row_max[:, s, two], -1.0, None,
                                              ALU.mult).then_inc(neg_ready, 1)
                        dve.wait_ge(exp_done, TB * (n + 1) + TB + 1)
                        dve.reciprocal(row_inv[:, s], row_sum[:, s]).then_inc(inv_ready, 1)
                        for c in (1, 3):
                            dve.wait_ge(turned, TB * n + c + 2)
                            dve.wait_ge(weighed, TB * n + c)
                            dve.tensor_copy(probsT[:, 1], turn_ps[:, 1, :]).then_inc(turned_b, 1)
                    dve.wait_ge(weighed, TB * HG * (it + 1) + 1)
                    out = aT[:, bass.ds(it // GROUPS * S, S)]
                    dve.tensor_tensor(out, out_ps[:, 0, :], out, ALU.add).then_inc(group_added, 1)


def output_projection_phase(nc, core, d, aT, Wo, bo):
    S, TB = d.S, d.TB
    with ExitStack() as ctx:
        def sb(name, shape):
            return ctx.enter_context(nc.sbuf_tensor("op_" + name, shape, F32))

        counted = []

        def sem(name):
            counted.append(ctx.enter_context(nc.semaphore("op_" + name)))
            return counted[-1]

        wo, b_row, ag = sb("wo", [P, P]), sb("b_row", [1, P]), sb("a_group", [P, 2, S])
        y_ps = ctx.enter_context(nc.psum_tensor("op_y_ps", [P, 2, TB, P], F32))
        loaded, ag_ready, y_done, y_added = sem("loaded"), sem("ag_ready"), sem("y_done"), sem("y_added")
        start_at_one(nc, counted, (loaded,))
        with nc.Block() as block:

            @block.sync
            def _(sp):
                sp.dma_start(wo[:], Wo).then_inc(loaded, 16)
                sp.dma_start(b_row[:], bo).then_inc(loaded, 16)

            @block.scalar
            def _(act):
                with act.Fori(0, d.B // 2) as gg:
                    for s in range(2):
                        g = gg * 2 + s
                        act.wait_ge(y_done, g + 1)
                        act.copy(ag[:, s], aT[:, bass.ds(g * S, S)]).then_inc(ag_ready, 1)

            @block.tensor
            def _(pe):
                pe.wait_ge(loaded, 32)
                with pe.Fori(0, d.B // 2) as gg:
                    for s in range(2):
                        g = gg * 2 + s
                        pe.wait_ge(ag_ready, g + 2)
                        pe.wait_ge(y_added, g + 1)
                        for t in range(TB):
                            pe.matmul(y_ps[:, s, t, :], ag[:, s, t * P:(t + 1) * P], wo[:], start=True, stop=False)
                            op = pe.matmul(y_ps[:, s, t, :], core.ones_row[:], b_row[:], start=False, stop=True)
                        op.then_inc(y_done, 1)

            @block.vector
            def _(dve):
                with dve.Fori(0, d.B // 2) as gg:
                    for s in range(2):
                        g = gg * 2 + s
                        dve.wait_ge(y_done, g + 2)
                        x = core.x[:, bass.ds(g * TB, TB), :]
                        dve.tensor_tensor(x, y_ps[:, s], x, ALU.add).then_inc(y_added, 1)


def store_phase(nc, core, d, out):
    with ExitStack() as ctx:
        stored = ctx.enter_context(nc.semaphore("stored"))
        with nc.Block() as block:

            @block.sync
            def _(sp):
                view = out.rearrange("(t p) c -> p t c", p=P)
                for q in range(4):
                    k = d.NT // 4
                    sp.dma_start(view[:, q * k:(q + 1) * k, :], core.x[:, q * k:(q + 1) * k, :]).then_inc(stored, 16)
                sp.wait_ge(stored, 64)


def two_layers(nc, a, out):
    d = Dims(a["x"], a["Wq0"], a["pos_emb"], a["Wg"], a["centroidT"], a["router_wT"], a["gate_all"])
    x_in = a["x"].rearrange("b s c -> (b s) c")
    with ExitStack() as ctx:
        core = Core(nc, ctx, d)
        setup_phase(nc, core, d, x_in)

        def route0(nc, core, d, scores):
            routing_phase(nc, core, d, "_r0", scores, core.gate0[:], 2, True)

        def route1(nc, core, d, scores):
            routing_phase(nc, core, d, "_r1", scores, core.gate1[:, :, 0:d.E1], 4, False)

        norm_phase(nc, core, d, "0", route0, a["centroidT"], None)
        cope_attention_phase(nc, core, d, "_a0", HOT0, a["Wq0"], a["Wkv"], a["Wout"], a["pos_emb"])
        hidden = [P] * (d.HC - 1) + [d.HL]
        moe_phase(nc, core, d, "_m0", a["Wg"], a["W1"], a["W2"], a["bg_cols"], a["b1_cols"], a["b2"], core.gate0, hidden)
        residual_phase(nc, core, d, a["b_out"])
        norm_phase(nc, core, d, "1", route1, a["router_wT"], a["router_bias"])
        with ExitStack() as inner:
            qT, kT, v, aT = (inner.enter_context(nc.sbuf_tensor("la_" + n, [P, d.T], F32)) for n in ("qT", "kT", "v", "aT"))
            biases = {n: a["b" + n] for n in "qklv"}
            latent_projection_phase(nc, core, d, qT, kT, v, a["Wq1"], a["Wl"], a["Wk"], a["Wv"], biases)
            latent_attention_phase(nc, core, d, qT, kT, v, aT)
            output_projection_phase(nc, core, d, aT, a["Wo"], a["bo"])
        moe_phase(nc, core, d, "_m1", a["gate_all"], a["up_all"], a["down_all"], None, None, None, core.gate1, [P])
        store_phase(nc, core, d, out)


HOT0 = 512


def lay_out(np, inp):
    f = {k: np.asarray(v) for k, v in inp.items()}
    A = np.ascontiguousarray
    E, _, H = f["L0_ffn_Wg"].shape
    D = f["L0_attn_x"].shape[-1]
    HC = -(-H // D)

    def columns(b):
        padded = np.zeros((E, HC * D), b.dtype)
        padded[:, :H] = b
        return A(padded.reshape(E, HC, D).transpose(0, 2, 1))

    def shared(w):
        return w.reshape(-1, D, D)

    gate = np.concatenate([f["L1_ffn_gate_w"], shared(f["L1_ffn_sgate_w"])])
    up = np.concatenate([f["L1_ffn_up_w"], shared(f["L1_ffn_sup_w"])])
    down = np.concatenate([f["L1_ffn_down_w"].transpose(0, 2, 1), shared(A(f["L1_ffn_sdown_w"].T))])
    return dict(
        x=A(f["L0_attn_x"][:, ::-1]), Wq0=f["L0_attn_Wq"], Wkv=f["L0_attn_Wkv"], Wout=f["L0_attn_Wout"],
        b_out=f["L0_attn_b_out"][None], pos_emb=f["L0_attn_pos_emb"], centroidT=A(f["L0_ffn_centroid"].T),
        Wg=f["L0_ffn_Wg"], W1=f["L0_ffn_W1"], W2=f["L0_ffn_W2"], bg_cols=columns(f["L0_ffn_bg"]),
        b1_cols=columns(f["L0_ffn_b1"]), b2=f["L0_ffn_b2"], Wq1=f["L1_attn_Wq"], Wl=f["L1_attn_Wl"],
        Wk=f["L1_attn_Wk"], Wv=f["L1_attn_Wv"], Wo=f["L1_attn_Wo"], bq=A(f["L1_attn_bq"][:, None]),
        bl=A(f["L1_attn_bl"][:, None]), bk=A(f["L1_attn_bk"][:, None]), bv=f["L1_attn_bv"][None],
        bo=f["L1_attn_bo"][None], router_wT=A(f["L1_ffn_router_w"].T), router_bias=f["L1_ffn_router_bias"][None],
        gate_all=A(gate.transpose(0, 2, 1)), up_all=A(up.transpose(0, 2, 1)), down_all=A(down))


def kernel(**inputs):
    import numpy as _np
    import concourse.bacc as _bacc
    from concourse import mybir as _mybir
    from concourse.bass_utils import run_bass_kernel_spmd as _run

    nc = _bacc.Bacc("TRN2", target_bir_lowering=False, num_devices=1)
    arrays, args = {}, {}
    for name, a in lay_out(_np, inputs).items():
        arrays[name + "_dram"] = a
        args[name] = nc.dram_tensor(name + "_dram", a.shape, _mybir.dt.from_np(a.dtype), kind="ExternalInput").ap()
    B, S, D = inputs["L0_attn_x"].shape
    out = nc.dram_tensor("out_dram", (B * S, D), F32, kind="ExternalOutput").ap()
    two_layers(nc, args, out)
    r = _run(nc, [arrays], core_ids=[0])
    return _np.ascontiguousarray(r.results[0]["out_dram"].reshape(B, S, D)[:, ::-1])
```

```python
from contextlib import ExitStack, nullcontext

import concourse.bass as bass
from concourse import mybir

F32 = mybir.dt.float32
BF16 = mybir.dt.bfloat16
I16 = mybir.dt.int16
U32 = mybir.dt.uint32
I32 = mybir.dt.int32
F32R = mybir.dt.float32r
ALU = mybir.AluOpType
ACT = mybir.ActivationFunctionType
AX = mybir.AxisListType

P = 128


class Dims:

    def __init__(self, x, Wq, pos_emb, Wg, centroid, router_w, gate_all):
        self.B, self.S, self.D = x.shape
        self.T = self.B * self.S
        self.NT = self.T // P
        self.TB = self.S // P
        self.DH, self.TMAX = pos_emb.shape
        self.HEADS = Wq.shape[1] // self.DH
        self.PAIRS = self.HEADS // 2
        self.E0, _, self.H0 = Wg.shape
        self.HC = -(-self.H0 // P)
        self.HL = self.H0 - P * (self.HC - 1)
        self.E1 = router_w.shape[1]
        self.EA = gate_all.shape[0]
        self.HEADS1 = 16
        self.DH1 = self.D // self.HEADS1
        assert self.D == P and self.S == 512 and self.DH == 64 and self.TMAX == 64


class Core:

    def __init__(self, nc, ctx, d):
        def sb(name, shape, dt=F32):
            return ctx.enter_context(nc.sbuf_tensor(name, shape, dt))

        self.x = sb("x_tokens", [P, d.NT, P])
        self.xnT = sb("xn_T", [P, d.T])
        self.attn = sb("attn_out", [P, d.NT, P])
        self.gate0 = sb("gate0", [P, d.NT, d.E0])
        self.gate1 = sb("gate1", [P, d.NT, d.EA])
        self.ident = sb("ident", [P, P])
        self.ones_row = sb("ones_row", [1, P])
        self.reached = sb("reached", [P, d.TB])
        self.redo = sb("redo", [1, 1], I32)
        self.ones_col = sb("ones_col", [P, 1])


def start_at_one(nc, semaphores, loads):
    with nc.Block() as block:

        @block.sync
        def _(sp):
            for s in semaphores:
                if all(s is not x for x in loads):
                    sp.sem_inc(s, 1)


def setup_phase(nc, core, d, x_in):
    with ExitStack() as ctx:
        x_loaded = ctx.enter_context(nc.semaphore("x_loaded"))
        filled = ctx.enter_context(nc.semaphore("const_filled"))
        block = ctx.enter_context(nc.Block())

        @block.sync
        def _(sp):
            view = x_in.rearrange("(t p) c -> p t c", p=P)
            for q in range(4):
                k = d.NT // 4
                sp.dma_start(core.x[:, q * k:(q + 1) * k, :], view[:, q * k:(q + 1) * k, :]).then_inc(x_loaded, 16)
            sp.wait_ge(x_loaded, 64)

        @block.gpsimd
        def _(pool):
            pool.memset(core.ident[:], 0.0).then_inc(filled, 1)
            pool.memset(core.ones_row[:], 1.0).then_inc(filled, 1)
            pool.memset(core.ones_col[:], 1.0).then_inc(filled, 1)
            pool.memset(core.reached[:], float(d.TMAX - 1)).then_inc(filled, 1)
            pool.memset(core.gate1[:, :, d.E1:d.EA], 1.0).then_inc(filled, 1)
            pool.wait_ge(filled, 5)
            pool.affine_select(out=core.ident[:], in_=core.ident[:], compare_op=ALU.not_equal, fill=1.0,
                               base=0, pattern=[[-1, P]], channel_multiplier=1).then_inc(filled, 1)
            pool.wait_ge(filled, 6)


def norm_phase(nc, core, d, tag, router, router_rhs_in, router_row_in):
    distances = tag == "0"
    NE = d.E0 if distances else d.E1
    TB, NT = d.TB, d.NT
    with ExitStack() as ctx:
        def sb(name, shape, dt=F32):
            return ctx.enter_context(nc.sbuf_tensor(name + tag, shape, dt))

        counted = []

        def sem(name):
            counted.append(ctx.enter_context(nc.semaphore(name + tag)))
            return counted[-1]

        stats = sb("bn_stats", [P, 2, TB, 6])
        mean_var = sb("mean_var", [P, 2, TB, 2])
        std = sb("std", [P, 2, TB])
        rstd = sb("rstd", [P, 2, TB])
        xn = sb("xn", [P, 2, TB, P])
        square = sb("square", [P, TB, P])
        sumsq = sb("sumsq", [P, 2, TB])
        xg = sb("xn_T_group", [P, 2, TB * P])
        rhs = sb("router_rhs", [P, NE])
        row = sb("router_row", [1, NE])
        scores = sb("scores", [P, NT, NE])
        eps = sb("eps", [P, 1])
        turned = ctx.enter_context(nc.psum_tensor("turned" + tag, [P, 2, TB, P], F32))
        score_ps = ctx.enter_context(nc.psum_tensor("score_ps" + tag, [P, 2, 512], F32))

        router_loaded = sem("router_loaded")
        router_ready = sem("router_ready")
        eps_ready, wait_carried = sem("eps_ready"), sem("wait_carried")
        stats_done, aggr_done, std_done, rstd_done = sem("stats"), sem("aggr"), sem("std_s"), sem("rstd_s")
        xn_done, sq_done, turned_done, xg_done = sem("xn_s"), sem("sq_s"), sem("turned_s"), sem("xg_s")
        xnT_done, score_done, score_out = sem("xnT_s"), sem("score_s"), sem("score_out")
        start_at_one(nc, counted, (router_loaded,))

        def lagged(eng, first, second):
            first(0, 0)
            with eng.Fori(0, d.B // 2 - 1) as k:
                first(k * 2 + 1, 1)
                second(k * 2, 0)
                first(k * 2 + 2, 0)
                second(k * 2 + 1, 1)
            first(d.B - 1, 1)
            second(d.B - 2, 0)
            second(d.B - 1, 1)

        with nc.Block() as block:

            @block.sync
            def _(sp):
                sp.dma_start(rhs[:], router_rhs_in).then_inc(router_loaded, 16)
                if not distances:
                    sp.dma_start(row[:], router_row_in).then_inc(router_loaded, 16)

            @block.vector
            def _(dve):
                dve.memset(eps[:], 1e-5).then_inc(eps_ready, 1)
                if distances:
                    dve.wait_ge(router_loaded, 16)
                    dve.tensor_tensor(square[:, 0, 0:NE], rhs[:], rhs[:], ALU.mult).then_inc(router_ready, 1)
                    dve.wait_ge(router_ready, 2)
                    dve.tensor_scalar(rhs[:], rhs[:], -2.0, None, ALU.mult).then_inc(router_ready, 1)
                    dve.wait_ge(router_ready, 4)
                    dve.tensor_copy(row[:], score_ps[0:1, 0, 0:NE]).then_inc(router_ready, 1)

                def normalise(g, s):
                    for t in range(TB):
                        dve.bn_stats(stats[:, s, t, :], core.x[:, bass.ds(g * TB + t, 1), :]).then_inc(stats_done, 1)
                    dve.wait_ge(stats_done, (g + 1) * TB + 1)
                    dve.sem_inc(wait_carried, 1)
                    for t in range(TB):
                        dve.bn_aggr(mean_var[:, s, t, :], stats[:, s, t, :]).then_inc(aggr_done, 1)
                    dve.wait_ge(std_done, g + 2)
                    dve.reciprocal(rstd[:, s, :], std[:, s, :]).then_inc(rstd_done, 1)
                    dve.wait_ge(rstd_done, g + 2)
                    dve.wait_ge(turned_done, g * TB + 1)
                    for t in range(TB):
                        dve.tensor_scalar(xn[:, s, t, :], core.x[:, bass.ds(g * TB + t, 1), :],
                                          mean_var[:, s, t, 0:1], rstd[:, s, t:t + 1],
                                          ALU.subtract, ALU.mult).then_inc(xn_done, 1)

                def keep(g, s):
                    dve.wait_ge(xg_done, g + 2)
                    dve.tensor_copy(core.xnT[:, bass.ds(g * TB * P, TB * P)], xg[:, s, :]).then_inc(xnT_done, 1)
                    dve.wait_ge(score_done, g + 2)
                    psv = score_ps[:, s, 0:TB * NE].rearrange("p (t e) -> p t e", t=TB)
                    if distances:
                        dve.wait_ge(sq_done, (g + 1) * TB + 1)
                        for t in range(TB):
                            op = dve.tensor_scalar(scores[:, bass.ds(g * TB + t, 1), :], psv[:, t, :],
                                                   sumsq[:, s, t:t + 1], 1e-12, ALU.add, ALU.max)
                    else:
                        op = dve.tensor_copy(scores[:, bass.ds(g * TB, TB), :], psv)
                    op.then_inc(score_out, 1)

                lagged(dve, normalise, keep)

            @block.scalar
            def _(act):
                act.wait_ge(eps_ready, 2)

                def deviation(g, s):
                    act.wait_ge(aggr_done, (g + 1) * TB + 1)
                    act.activation(std[:, s, :], mean_var[:, s, :, 1], ACT.Sqrt, bias=eps[:]).then_inc(std_done, 1)

                def keep(g, s):
                    if distances:
                        act.wait_ge(xn_done, (g + 1) * TB + 1)
                        act.wait_ge(sq_done, g * TB + 1)
                        for t in range(TB):
                            act.activation(square[:, t, :], xn[:, s, t, :], ACT.Square,
                                           accum_out=sumsq[:, s, t:t + 1]).then_inc(sq_done, 1)
                    act.wait_ge(turned_done, (g + 1) * TB + 1)
                    act.copy(xg[:, s, :], turned[:, s, :, :]).then_inc(xg_done, 1)

                lagged(act, deviation, keep)

            @block.tensor
            def _(pe):
                if distances:
                    pe.wait_ge(router_ready, 3)
                    pe.matmul(score_ps[0:1, 0, 0:NE], core.ones_col[:], square[:, 0, 0:NE], start=True,
                              stop=True).then_inc(router_ready, 1)
                    pe.wait_ge(router_ready, 5)
                else:
                    pe.wait_ge(router_loaded, 32)

                def turn(g, s):
                    pe.wait_ge(xn_done, (g + 1) * TB + 1)
                    pe.wait_ge(xg_done, g + 1)
                    for t in range(TB):
                        pe.transpose(turned[:, s, t, :], xn[:, s, t, :], core.ident[:]).then_inc(turned_done, 1)

                def score(g, s):
                    pe.wait_ge(xg_done, g + 2)
                    pe.wait_ge(score_out, g + 1)
                    for t in range(TB):
                        out = score_ps[:, s, t * NE:(t + 1) * NE]
                        pe.matmul(out, xg[:, s, t * P:(t + 1) * P], rhs[:], start=True, stop=False)
                        op = pe.matmul(out, core.ones_row[:], row[:], start=False, stop=True)
                    op.then_inc(score_done, 1)

                with pe.Fori(0, d.B // 2) as gg:
                    for s in range(2):
                        turn(gg * 2 + s, s)
                        score(gg * 2 + s, s)

        router(nc, core, d, scores)


def routing_phase(nc, core, d, tag, scores, gates, topk, distances):
    NT, NE = scores.shape[1], scores.shape[2]
    with ExitStack() as ctx:
        def sb(name, shape, dt=F32):
            return ctx.enter_context(nc.sbuf_tensor(name + tag, shape, dt))

        best = sb("best8", [P, NT, 8])
        where = sb("where8", [P, NT, 8], U32)
        where_f = sb("where8_f", [P, NT, 8])
        numbers = sb("expert_numbers", [P, NE])
        hit = sb("hit", [P, NT, NE])
        picked = sb("picked", [P, NT, NE])
        top = sb("row_max", [P, NT])
        total = sb("row_sum", [P, NT])
        inv = sb("row_inv", [P, NT])
        step = ctx.enter_context(nc.semaphore("route_step" + tag))
        activated = ctx.enter_context(nc.semaphore("route_act" + tag))
        numbered = ctx.enter_context(nc.semaphore("route_numbers" + tag))
        shift_done = ctx.enter_context(nc.semaphore("route_shift" + tag))

        def wide(a):
            return a.unsqueeze(2).to_broadcast([P, NT, NE])

        with nc.Block() as block:

            @block.gpsimd
            def _(pool):
                pool.iota(numbers[:], pattern=[[1, NE]], base=0, channel_multiplier=0,
                          allow_small_or_imprecise_dtypes=True).then_inc(numbered, 1)

            @block.scalar
            def _(act):
                if distances:
                    act.activation(scores[:], scores[:], ACT.Sqrt).then_inc(activated, 1)
                act.wait_ge(shift_done, 1)
                act.activation(picked[:], picked[:], ACT.Exp).then_inc(activated, 1)

            @block.vector
            def _(dve):
                n = [0]

                def done(op):
                    op.then_inc(step, 1)
                    n[0] += 1
                    dve.wait_ge(step, n[0])

                a = 0
                if distances:
                    a = 1
                    dve.wait_ge(activated, 1)
                done(dve.tensor_reduce(top[:], scores[:], AX.X, ALU.max))
                dve.tensor_tensor(picked[:], scores[:], wide(top[:]), ALU.subtract).then_inc(shift_done, 1)
                dve.wait_ge(activated, a + 1)
                if not distances:
                    done(dve.tensor_reduce(total[:], picked[:], AX.X, ALU.add))
                    done(dve.reciprocal(inv[:], total[:]))
                    done(dve.tensor_tensor(scores[:], picked[:], wide(inv[:]), ALU.mult))
                    done(dve.tensor_copy(picked[:], scores[:]))
                for t in range(NT):
                    op = dve.max(best[:, t, :], scores[:, t, :])
                done(op)
                for t in range(NT):
                    op = dve.max_index(where[:, t, :], best[:, t, :], scores[:, t, :])
                done(op)
                done(dve.tensor_copy(where_f[:], where[:]))
                dve.wait_ge(numbered, 1)
                num = numbers[:].unsqueeze(1).to_broadcast([P, NT, NE])
                for k in range(topk):
                    out = gates if k == 0 else hit[:]
                    done(dve.tensor_tensor(out, num, wide(where_f[:, :, k]), ALU.is_equal))
                    if k:
                        done(dve.tensor_tensor(gates, gates, hit[:], ALU.add))
                done(dve.tensor_tensor(picked[:], picked[:], gates, ALU.mult))
                done(dve.tensor_reduce(total[:], picked[:], AX.X, ALU.add))
                if not distances:
                    done(dve.tensor_scalar(total[:], total[:], 1e-12, None, ALU.max))
                done(dve.reciprocal(inv[:], total[:]))
                done(dve.tensor_tensor(gates, picked[:], wide(inv[:]), ALU.mult))


def moe_phase(nc, core, d, tag, Wg, W1, W2, bias_g, bias_1, bias_2, gates, hidden):
    NE = Wg.shape[0]
    HC, HL = len(hidden), hidden[-1]
    H = sum(hidden)
    biased = bias_g is not None
    ONE = 96
    K = [h for h in hidden[:-1]] + [ONE + 1 if biased else HL]
    G, TB = d.B, d.TB
    N = TB * P
    assert NE % 2 == 0 and (not biased or HL <= ONE)
    with ExitStack() as ctx:
        def sb(name, shape, dt=F32):
            return ctx.enter_context(nc.sbuf_tensor(name + tag, shape, dt))

        def sem(name):
            return ctx.enter_context(nc.semaphore(name + tag))

        wg = [sb(f"wg{s}_", [P, H]) for s in range(2)]
        w1 = [sb(f"w1{s}_", [P, H]) for s in range(2)]
        w2 = [sb(f"w2{s}_", [P, HC, P]) for s in range(2)]
        bg = [sb(f"bg{s}_", [P, HC]) for s in range(2)]
        b1 = [sb(f"b1{s}_", [P, HC]) for s in range(2)]
        wg_parts = [sb(f"wg_parts{s}_", [P, 2, H], F32R) for s in range(2)]
        w1_parts = [sb(f"w1_parts{s}_", [P, 2, H], F32R) for s in range(2)]
        x_parts = [sb(f"x_{n}_", [P, d.T], F32R) for n in ("hi", "lo")]
        silu = sb("silu", [P, 2, N])
        hT = sb("hT", [P, 2, HC, N])
        gate_ps = ctx.enter_context(nc.psum_tensor("gate_ps" + tag, [P, 2, N], F32))
        up_ps = ctx.enter_context(nc.psum_tensor("up_ps" + tag, [P, 2, N], F32))
        down_ps = ctx.enter_context(nc.psum_tensor("down_ps" + tag, [P, 2, TB, P], F32))
        w_loaded = [sem(f"w_loaded{s}_") for s in range(2)]
        w_free = [sem(f"w_free{s}_") for s in range(2)]
        gate_done, up_done, silu_done, h_done = sem("gate_s"), sem("up_s"), sem("silu_s"), sem("h_s")
        down_done, added = sem("down_s"), sem("added_s")
        ones_set = sem("ones_set")
        x_hi_ready, x_parts_ready = sem("x_hi_ready"), sem("x_parts_ready")
        w_hi_ready, w_parts_ready = sem("w_hi_ready"), sem("w_parts_ready")
        wait_carried = sem("wait_carried")
        LOADS = 7 if biased else 3
        LW = 16 * LOADS

        with nc.Block() as block:

            @block.sync
            def _(sp):
                if biased:
                    sp.wait_ge(ones_set, 4)
                with sp.Fori(0, NE // 2) as ee:
                    for s in range(2):
                        e = ee * 2 + s
                        sp.wait_ge(w_free[s], ee + 1)

                        def load(dst, src):
                            sp.dma_start(dst, src).then_inc(w_loaded[s], 16)

                        load(wg[s][:], Wg[bass.ds(e, 1)].rearrange("o k h -> k (o h)"))
                        load(w1[s][:], W1[bass.ds(e, 1)].rearrange("o k h -> k (o h)"))
                        if not biased:
                            load(w2[s][:, 0, :], W2[bass.ds(e, 1)].rearrange("o h c -> h (o c)"))
                        else:
                            F = (HC - 1) * P
                            w2e = W2[bass.ds(e, 1)].rearrange("o h c -> (o h) c")
                            load(w2[s][:, 0:HC - 1, :], w2e[0:F, :].rearrange("(k p) c -> p k c", p=P))
                            load(w2[s][0:HL, HC - 1, :], w2e[F:H, :])
                            load(w2[s][ONE:ONE + 1, HC - 1, :], bias_2[bass.ds(e, 1), :])
                            for dst, src in ((bg[s], bias_g), (b1[s], bias_1)):
                                load(dst[:], src[bass.ds(e, 1)].rearrange("o p k -> p (o k)"))

            @block.gpsimd
            def _(pool):
                for s in range(2):
                    pool.sem_inc(w_free[s], 1)
                if biased:
                    for s in range(2):
                        pool.memset(hT[:, s, HC - 1, :], 0.0).then_inc(ones_set, 1)
                        pool.memset(w2[s][:, HC - 1, :], 0.0).then_inc(ones_set, 1)
                    pool.wait_ge(ones_set, 4)
                    pool.memset(hT[ONE:ONE + 1, :, HC - 1, :], 1.0).then_inc(ones_set, 1)
                    pool.wait_ge(ones_set, 5)
                with pool.Fori(0, NE // 2) as ee:
                    for s in range(2):
                        e = ee * 2 + s
                        pool.wait_ge(w_loaded[s], (ee + 1) * LW)
                        pool.wait_ge(w_free[s], ee + 1)
                        pool.sem_inc(wait_carried, 1)
                        for parts, w in ((wg_parts[s], wg[s]), (w1_parts[s], w1[s])):
                            pool.tensor_scalar(parts[:, 0, :], w[:], 1.0, None, ALU.mult).then_inc(w_hi_ready, 1)
                        pool.wait_ge(w_hi_ready, 2 * (e + 1))
                        for parts, w in ((wg_parts[s], wg[s]), (w1_parts[s], w1[s])):
                            pool.tensor_tensor(parts[:, 1, :], w[:], parts[:, 0, :], ALU.subtract).then_inc(w_parts_ready, 1)

            def groups_lagged(eng, first, second, ee, s):
                def at(g, r):
                    return g, r, (ee * 2 + s) * G + g
                first(*at(0, 0))
                with eng.Fori(0, G // 2 - 1) as k:
                    first(*at(k * 2 + 1, 1))
                    second(*at(k * 2, 0))
                    first(*at(k * 2 + 2, 0))
                    second(*at(k * 2 + 1, 1))
                first(*at(G - 1, 1))
                second(*at(G - 2, 0))
                second(*at(G - 1, 1))

            @block.tensor
            def _(pe):
                if biased:
                    pe.wait_ge(ones_set, 5)
                pe.wait_ge(x_parts_ready, G)
                with pe.Fori(0, NE // 2) as ee:
                    for s in range(2):
                        pe.wait_ge(w_loaded[s], (ee + 1) * LW)
                        pe.wait_ge(w_parts_ready, 2 * (ee * 2 + s + 1))

                        def product(out, parts, cols, g):
                            for w, x in ((0, 0), (0, 1), (1, 0)):
                                op = pe.matmul(out, parts[:, w, cols], x_parts[x][:, bass.ds(g * N, N)],
                                               start=(w + x == 0), stop=(w == 1))
                            return op

                        def gate_up(g, r, n):
                            for c in range(HC):
                                slot = (r * HC + c) % 2
                                pe.wait_ge(h_done, n * HC + c + 1)
                                cols = slice(c * P, c * P + hidden[c])
                                product(gate_ps[0:hidden[c], slot, :], wg_parts[s], cols, g).then_inc(gate_done, 1)
                                product(up_ps[0:hidden[c], slot, :], w1_parts[s], cols, g).then_inc(up_done, 1)

                        def down(g, r, n):
                            pe.wait_ge(h_done, (n + 1) * HC + 2)
                            pe.wait_ge(added, n + 1)
                            for t in range(TB):
                                for c in range(HC):
                                    op = pe.matmul(down_ps[:, r, t, :], hT[0:K[c], r, c, t * P:(t + 1) * P],
                                                   w2[s][0:K[c], c, :], start=(c == 0), stop=(c == HC - 1))
                            op.then_inc(down_done, 1)

                        groups_lagged(pe, gate_up, down, ee, s)

            @block.scalar
            def _(act):
                for g in range(G):
                    act.copy(x_parts[0][:, g * N:(g + 1) * N], core.xnT[:, g * N:(g + 1) * N]).then_inc(x_hi_ready, 1)
                with act.Fori(0, NE // 2) as ee:
                    for s in range(2):
                        if biased:
                            act.wait_ge(w_loaded[s], (ee + 1) * LW)
                        with act.Fori(0, G // 2) as gg:
                            for r in range(2):
                                n = (ee * 2 + s) * G + gg * 2 + r
                                for c in range(HC):
                                    slot = (r * HC + c) % 2
                                    rows = hidden[c]
                                    act.wait_ge(gate_done, n * HC + c + 1)
                                    act.wait_ge(h_done, n * HC + c + 1)
                                    if biased:
                                        op = act.activation(silu[0:rows, slot, :], gate_ps[0:rows, slot, :], ACT.Silu,
                                                            bias=bg[s][0:rows, c:c + 1])
                                    else:
                                        op = act.activation(silu[0:rows, slot, :], gate_ps[0:rows, slot, :], ACT.Silu)
                                    op.then_inc(silu_done, 1)

            @block.vector
            def _(dve):
                for g in range(G):
                    dve.wait_ge(x_hi_ready, g + 1)
                    tokens = slice(g * N, (g + 1) * N)
                    dve.tensor_tensor(x_parts[1][:, tokens], core.xnT[:, tokens], x_parts[0][:, tokens],
                                      ALU.subtract).then_inc(x_parts_ready, 1)
                for free in (h_done, h_done, added, added):
                    dve.sem_inc(free, 1)
                with dve.Fori(0, NE // 2) as ee:
                    for s in range(2):
                        def hidden_product(g, r, n):
                            for c in range(HC):
                                slot = (r * HC + c) % 2
                                rows = hidden[c]
                                dve.wait_ge(silu_done, n * HC + c + 1)
                                dve.wait_ge(up_done, n * HC + c + 1)
                                h, u, z = hT[0:rows, r, c, :], up_ps[0:rows, slot, :], silu[0:rows, slot, :]
                                if biased:
                                    op = dve.scalar_tensor_tensor(out=h, in0=u, scalar=b1[s][0:rows, c:c + 1],
                                                                  in1=z, op0=ALU.add, op1=ALU.mult)
                                else:
                                    op = dve.tensor_tensor(h, u, z, ALU.mult)
                                op.then_inc(h_done, 1)

                        def add(g, r, n):
                            e = ee * 2 + s
                            dve.wait_ge(down_done, n + 1)
                            for t in range(TB):
                                xt = core.x[:, bass.ds(g * TB + t, 1), :].rearrange("p o c -> p (o c)")
                                we = gates[:, bass.ds(g * TB + t, 1), bass.ds(e, 1)].rearrange("p o c -> p (o c)")
                                op = dve.scalar_tensor_tensor(out=xt, in0=down_ps[:, r, t, :], scalar=we, in1=xt,
                                                              op0=ALU.mult, op1=ALU.add)
                            op.then_inc(added, 1)

                        groups_lagged(dve, hidden_product, add, ee, s)
                        dve.sem_inc(w_free[s], 1)


def cope_attention_phase(nc, core, d, tag, HOT, condition, x_in, Wq, Wkv, Wout, pos_emb):
    S, TB, DH, TM = d.S, d.TB, d.DH, d.TMAX
    H1 = HOT + 1
    UNITS = d.B * d.HEADS
    BITS = (32, 16, 8, 4, 2, 1)
    NTAB = TM + 2
    scale = DH ** -0.5
    with ExitStack() as ctx:
        def sb(name, shape, dt=F32):
            return ctx.enter_context(nc.sbuf_tensor(name + tag, shape, dt))

        def ps(name, shape):
            return ctx.enter_context(nc.psum_tensor(name + tag, shape, F32))

        counted = []

        def sem(name):
            counted.append(nc.alloc_semaphore(name=name + tag))
            return counted[-1]

        wqk = sb("wqk", [P, 2, P])
        wv = sb("wv", [P, P])
        wout = sb("wout", [P, 2, P])
        table_w = sb("table_w", [P, 2, P])
        pe_raw = sb("pe_raw", [P, TM])
        xb = sb("x_batch", [P, S])
        qT = sb("qT", [P, S])
        kT = sb("kT", [P, 2, S])
        v = sb("v", [P, TB, P])
        logits = sb("logits", [P, 3, TB, S])
        probs = core.x if x_in is not None else sb("probs", [P, 2 * TB * TB, P])
        g_sig = sb("g_sig", [P, 2, TB, H1])
        slope = sb("slope", [P, 2, TB, HOT])
        ends = sb("table_ends", [P, 2, TB, 2])
        pos = sb("pos", [P, TB, H1])
        n_raw = sb("n_raw", [P, TB, H1], I16)
        n_pos = sb("n_pos", [P, TB, H1], BF16)
        shift = n_raw
        masks = sb("masks", [P, 3, TB, H1], I16)
        frac = sb("frac", [P, TB, HOT])
        stepped = sb("stepped", [P, TB, HOT], BF16)
        gain = sb("gain", [P, TB, H1])
        e_floor = sb("e_floor", [P, TB, H1])
        row_max = sb("row_max", [P, TB])
        neg_max = sb("neg_max", [P, 2, TB])
        row_sum = sb("row_sum", [P, 2, TB])
        row_inv = sb("row_inv", [P, 2, TB])
        diag = sb("diag", [P, TB, P])
        probsT = sb("probsT", [P, TB, TB, P])
        outT = sb("outT", [P, 2, S])
        y_sb = sb("y", [P, TB, P])
        cap = sb("cap", [P, TB, H1], BF16)
        keep = sb("keep", [P, TB, H1], BF16)
        one = sb("one", [P, 1], BF16)
        key = sb("key", [P, 1, H1], I16)

        scores_ps = ps("scores_ps", [P, TB, S])
        small_ps = ps("small_ps", [P, S])
        turn_ps = ps("turn_ps", [P, 2, S])
        out_ps = ps("out_ps", [P, S])

        wqk_loaded, wv_loaded = sem("wqk_loaded"), sem("wv_loaded")
        wout_loaded, pe_loaded, x_loaded = sem("wout_loaded"), sem("pe_loaded"), sem("x_loaded")
        const_done = sem("const_done")
        table_step = sem("table_step")
        xb_ready, q_done, k_done, v_done = sem("xb_ready"), sem("q_done"), sem("k_done"), sem("v_done")
        qT_ready, kT_ready, v_ready = sem("qT_ready"), sem("kT_ready"), sem("v_ready")
        y_kept, y_added = sem("y_kept"), sem("y_added")
        scores_done, table_done, logits_ready = sem("scores_done"), sem("table_done"), sem("logits_ready")
        tanh_done, g_ready, slope_ready = sem("tanh_done"), sem("g_ready"), sem("slope_ready")
        pos_ready, n_raw_ready, n_ready, shift_ready = sem("pos_r"), sem("n_raw_r"), sem("n_r"), sem("shift_r")
        mask_ready, slope_step = sem("mask_r"), sem("slope_step")
        frac_ready, stepped_ready, gain_ready = sem("frac_r"), sem("stepped_r"), sem("gain_r")
        floor_ready, rise_ready, cope_ready = sem("floor_r"), sem("rise_r"), sem("cope_r")
        logits_hot, max_ready, neg_ready = sem("logits_hot"), sem("max_r"), sem("neg_r")
        exp_done, inv_ready, diag_ready = sem("exp_done"), sem("inv_r"), sem("diag_r")
        turned, probs_ready, out_done, outT_ready = sem("turned_p"), sem("probs_r"), sem("out_done"), sem("outT_r")
        y_done = sem("y_done")
        reach_kept = sem("reach_kept")
        wait_carried, pool_wait_carried = sem("wait_carried"), sem("pool_wait_carried")

        def flat(t):
            return t.rearrange("p b h -> p (b h)")

        def chunk(h, b, c):
            return probs[:, (h * TB + b) * TB + c, :]

        def exists(m):
            return not isinstance(m, int) or 0 <= m < UNITS

        start_at_one(nc, counted, (wqk_loaded, wv_loaded, wout_loaded, pe_loaded, x_loaded))

        def when(eng):
            if condition is None:
                return nullcontext()
            return eng.If(eng.value_load(condition, min_val=0, max_val=1) != 0)

        PAIRS = UNITS // 2
        LEAD, TRAIL = 2, 2

        def all_steps(eng, step):
            def steps(pair, number):
                for h in range(2):
                    step(pair, h, (2 * number + h) % 3)

            for pair in range(-1, LEAD):
                steps(pair, pair)
            with eng.Fori(0, (PAIRS - LEAD - TRAIL) // 3) as triple:
                for i in range(3):
                    steps(triple * 3 + LEAD + i, LEAD + i)
            for pair in range(PAIRS - TRAIL, PAIRS + 2):
                steps(pair, pair)

        with nc.Block() as block:

            @block.sync
            def _(sp):
                def weights(p):
                    if exists(p * 2):
                        col = p % d.PAIRS * P
                        if exists(p * 2 - 2):
                            sp.wait_ge(k_done, p + 1)
                        for i, w in enumerate((Wq, Wkv)):
                            sp.dma_start(wqk[:, i, :], w[:, bass.ds(col, P)]).then_inc(wqk_loaded, 16)
                    if exists(p * 2 - 2):
                        col = (p - 1) % d.PAIRS * P
                        if exists(p * 2 - 4):
                            sp.wait_ge(v_done, p)
                        sp.dma_start(wv[:], Wkv[:, bass.ds(d.HEADS * DH + col, P)]).then_inc(wv_loaded, 16)
                    if exists(p * 2 - 4):
                        row = (p - 2) % d.PAIRS * P
                        if exists(p * 2 - 6):
                            sp.wait_ge(y_done, p - 1)
                        for h in range(2):
                            for half in range(2):
                                sp.dma_start(wout[half * DH:(half + 1) * DH, h, :],
                                             Wout[bass.ds(row + h * DH, DH), :]).then_inc(wout_loaded, 16)

                with when(sp):
                    sp.dma_start(pe_raw[0:DH, :], pos_emb).then_inc(pe_loaded, 16)
                    sp.dma_start(pe_raw[DH:2 * DH, :], pos_emb).then_inc(pe_loaded, 16)
                    for p in range(3):
                        weights(p)
                    with sp.Fori(3, PAIRS) as p:
                        weights(p)
                    weights(PAIRS)
                    weights(PAIRS + 1)
                    if x_in is not None:
                        sp.wait_ge(turned, TB * UNITS + 1)
                        view = x_in.rearrange("(t p) c -> p t c", p=P)
                        for q in range(4):
                            t = slice(q * d.NT // 4, (q + 1) * d.NT // 4)
                            sp.dma_start(core.x[:, t, :], view[:, t, :]).then_inc(x_loaded, 16)
                        sp.wait_ge(x_loaded, 64)

            @block.gpsimd
            def _(pool):
                with when(pool):
                    pool.memset(core.attn[:], 0.0).then_inc(const_done, 1)
                    pool.memset(flat(cap[:]), float(TM - 1)).then_inc(const_done, 1)
                    pool.memset(flat(keep[:]), 1.0).then_inc(const_done, 1)
                    pool.memset(one[:], 1.0).then_inc(const_done, 1)
                    pool.iota(key[:], pattern=[[0, 1], [1, H1]], base=-1, channel_multiplier=0,
                              allow_small_or_imprecise_dtypes=True).then_inc(const_done, 1)
                    pool.wait_ge(const_done, 6)
                    pool.memset(cap[:, :, 0:1], 0.0).then_inc(const_done, 1)
                    pool.memset(keep[:, :, 0:1], 0.0).then_inc(const_done, 1)
                    for s in range(2):
                        pool.memset(g_sig[:, s, :, 0:1], 0.0).then_inc(const_done, 1)
                    pool.memset(gain[:], 0.0).then_inc(const_done, 1)
                    pool.memset(kT[:], 0.0).then_inc(const_done, 1)
                    pool.wait_ge(const_done, 12)

                    def add_cope(m):
                        pool.wait_ge(floor_ready, m + 2)
                        pool.wait_ge(rise_ready, m + 2)
                        pool.tensor_tensor(e_floor[:, :, 1:H1], frac[:], e_floor[:, :, 1:H1],
                                           ALU.add).then_inc(cope_ready, 1)

                    def spread_inverse(m, h):
                        pool.wait_ge(inv_ready, m + 2)
                        if exists(m - 1):
                            pool.wait_ge(turned, TB * m + 1)
                        pool.tensor_tensor(diag[:], core.ident[:].unsqueeze(1).to_broadcast([P, TB, P]),
                                           row_inv[:, h].unsqueeze(2).to_broadcast([P, TB, P]),
                                           ALU.mult).then_inc(diag_ready, 1)

                    def steps_and_fraction(n):
                        pool.wait_ge(n_ready, n + 2)
                        pool.tensor_tensor(stepped[:], n_pos[:, :, 1:H1], n_pos[:, :, 0:HOT],
                                           ALU.subtract).then_inc(stepped_ready, 1)
                        pool.wait_ge(cope_ready, n + 1)
                        pool.tensor_tensor(frac[:], pos[:, :, 1:H1], n_pos[:, :, 1:H1],
                                           ALU.subtract).then_inc(frac_ready, 1)

                    def passed(n, h):
                        pool.wait_ge(slope_step, (n + 1) * len(BITS) + 1)
                        pool.wait_ge(floor_ready, n + 1)
                        pool.sem_inc(pool_wait_carried, 1)
                        pool.tensor_copy(gain[:, :, 0:1], ends[:, h, :, 0:1]).then_inc(gain_ready, 1)
                        pool.wait_ge(stepped_ready, n + 2)
                        pool.tensor_tensor(gain[:, :, 2:H1], stepped[:, :, 1:HOT], slope[:, h, :, 0:HOT - 1],
                                           ALU.mult).then_inc(gain_ready, 1)
                        pool.wait_ge(frac_ready, n + 2)
                        pool.tensor_tensor(frac[:], frac[:], slope[:, h], ALU.mult).then_inc(rise_ready, 1)

                    def sigmoid(n, h):
                        pool.wait_ge(tanh_done, n + 2)
                        pool.sem_inc(pool_wait_carried, 1)
                        g = g_sig[:, h, :, 1:H1]
                        pool.tensor_scalar(g, g, 0.5, 0.5, ALU.mult, ALU.add).then_inc(g_ready, 1)

                    def add_output(p):
                        pool.wait_ge(y_kept, p + 2)
                        y = core.attn[:, bass.ds(p // d.PAIRS * TB, TB), :]
                        pool.tensor_tensor(y, y_sb[:], y, ALU.add).then_inc(y_added, 1)

                    def step(pair, h, k):
                        n = pair * 2 + h
                        if exists(n - 1):
                            add_cope(n - 1)
                        if exists(n - 2):
                            spread_inverse(n - 2, h)
                        if exists(n):
                            steps_and_fraction(n)
                        if exists(n + 1):
                            sigmoid(n + 1, 1 - h)
                        if h == 1 and exists(n - 5):
                            add_output(pair - 2)
                        if exists(n):
                            passed(n, h)

                    all_steps(pool, step)

            @block.vector
            def _(dve):
                with when(dve):
                    dve.wait_ge(pe_loaded, 32)
                    dve.memset(table_w[:], 0.0).then_inc(table_step, 1)
                    dve.wait_ge(table_step, 2)
                    for h in range(2):
                        own = slice(h * DH, (h + 1) * DH)
                        dve.tensor_tensor(table_w[own, h, 0:TM - 1], pe_raw[own, 1:TM], pe_raw[own, 0:TM - 1],
                                          ALU.subtract).then_inc(table_step, 1)
                        dve.tensor_copy(table_w[own, h, TM:TM + 1], pe_raw[own, 0:1]).then_inc(table_step, 1)
                        dve.tensor_copy(table_w[own, h, TM + 1:TM + 2], pe_raw[own, TM - 1:TM]).then_inc(table_step, 1)
                    dve.wait_ge(const_done, 12)

                    def positions(n, h):
                        dve.wait_ge(g_ready, n + 2)
                        dve.wait_ge(frac_ready, n + 1)
                        dve.tensor_tensor_scan(flat(pos[:]), flat(g_sig[:, h]), flat(cap[:]), 0.0,
                                               ALU.add, ALU.min).then_inc(pos_ready, 1)
                        dve.wait_ge(pos_ready, n + 2)
                        dve.tensor_scalar(flat(n_raw[:]), flat(pos[:]), -0.5, None, ALU.add).then_inc(n_raw_ready, 1)
                        if HOT < S:
                            dve.wait_ge(reach_kept, n + 1)
                            dve.tensor_tensor(core.reached[:].unsqueeze(2), core.reached[:].unsqueeze(2), pos[:, :, HOT:H1],
                                              ALU.min).then_inc(reach_kept, 1)
                        dve.wait_ge(n_raw_ready, n + 2)
                        dve.tensor_tensor_scan(flat(n_pos[:]), one[:].to_broadcast([P, TB * H1]), flat(n_raw[:]), -1.0,
                                               ALU.add, ALU.min).then_inc(n_ready, 1)

                    def sum_gains(m):
                        dve.wait_ge(gain_ready, 2 * (m + 1) + 1)
                        dve.wait_ge(logits_hot, m + 1)
                        dve.tensor_tensor_scan(flat(e_floor[:]), flat(keep[:]), flat(gain[:]), 0.0,
                                               ALU.mult, ALU.add).then_inc(floor_ready, 1)

                    def shifts(n):
                        dve.wait_ge(n_ready, n + 2)
                        dve.tensor_tensor(shift[:], key[:].to_broadcast([P, TB, H1]), n_pos[:],
                                          ALU.subtract).then_inc(shift_ready, 1)

                    def look_up(n, h, bits):
                        nb = len(BITS)

                        def mask(i):
                            dve.tensor_scalar(flat(masks[:, i % 3]), flat(shift[:]), BITS[i], None,
                                              ALU.bitwise_and).then_inc(mask_ready, 1)

                        if 0 in bits:
                            dve.wait_ge(shift_ready, n + 2)
                            mask(0)
                            dve.wait_ge(slope_ready, n + 2)
                        for i in bits:
                            if i + 1 < nb:
                                mask(i + 1)
                            far = BITS[i]
                            dve.wait_ge(mask_ready, n * nb + i + 2)
                            if i:
                                dve.wait_ge(slope_step, n * nb + i + 1)
                            dve.sem_inc(wait_carried, 1)
                            dve.copy_predicated(slope[:, h, :, far:HOT][:, :, ::-1], masks[:, i % 3, :, far + 1:H1][:, :, ::-1],
                                                slope[:, h, :, 0:HOT - far][:, :, ::-1]).then_inc(slope_step, 1)

                    def maxima(m, h, k):
                        dve.wait_ge(cope_ready, m + 2)
                        dve.wait_ge(logits_ready, m + 2)
                        hot = logits[:, k, :, 0:HOT]
                        dve.tensor_tensor(hot, hot, e_floor[:, :, 1:H1], ALU.add).then_inc(logits_hot, 1)
                        dve.wait_ge(logits_hot, m + 2)
                        dve.tensor_reduce(row_max[:], logits[:, k], AX.X, ALU.max).then_inc(max_ready, 1)
                        dve.wait_ge(max_ready, m + 2)
                        dve.tensor_scalar(neg_max[:, h], row_max[:], -1.0, None, ALU.mult).then_inc(neg_ready, 1)

                    def inverse_sum(m, h):
                        dve.wait_ge(exp_done, TB * (m + 1) + 1)
                        dve.reciprocal(row_inv[:, h], row_sum[:, h]).then_inc(inv_ready, 1)

                    def step(pair, h, k):
                        n = pair * 2 + h
                        if exists(n):
                            positions(n, h)
                        if exists(n - 1):
                            sum_gains(n - 1)
                        if exists(n):
                            shifts(n)
                            look_up(n, h, range(0, 3))
                        if exists(n - 2):
                            inverse_sum(n - 2, h)
                        if exists(n):
                            look_up(n, h, range(3, len(BITS)))
                        if exists(n - 1):
                            maxima(n - 1, 1 - h, (k + 2) % 3)

                    all_steps(dve, step)

            @block.scalar
            def _(act):
                with when(act):
                    act.wait_ge(const_done, 12)

                    def exponentials(m, h, k):
                        act.wait_ge(neg_ready, m + 2)
                        if exists(m - 2):
                            act.wait_ge(turned, TB * (m - 1) + 1)
                        for b in range(TB):
                            act.activation(probs[:, (h * TB + b) * TB:(h * TB + b + 1) * TB, :], logits[:, k, b, :], ACT.Exp,
                                           bias=neg_max[:, h, b:b + 1],
                                           accum_out=row_sum[:, h, b:b + 1]).then_inc(exp_done, 1)

                    def keep_scores(n, h, k):
                        act.wait_ge(scores_done, n + 2)
                        if exists(n - 3):
                            act.wait_ge(exp_done, TB * (n - 2) + 1)
                        op = act.activation(logits[:, k, :, 0:HOT], scores_ps[:, :, 0:HOT], ACT.Copy, scale=scale)
                        if HOT < S:
                            act.wait_ge(slope_ready, n + 2)
                            for b in range(TB):
                                op = act.activation(logits[:, k, b, HOT:S], scores_ps[:, b, HOT:S], ACT.Identity,
                                                    bias=ends[:, h, b, 1:2], scale=scale)
                        op.then_inc(logits_ready, 1)

                    def sigmoid(n, h):
                        act.wait_ge(scores_done, n + 2)
                        if exists(n - 2):
                            act.wait_ge(pos_ready, n)
                        act.activation(g_sig[:, h, :, 1:H1], scores_ps[:, :, 0:HOT], ACT.Tanh,
                                       scale=0.5 * scale).then_inc(tanh_done, 1)

                    def keep_table(n, h):
                        act.wait_ge(table_done, n + 2)
                        if exists(n - 2):
                            act.wait_ge(cope_ready, n)
                        tab = small_ps[:].rearrange("p (b t) -> p b t", b=TB)
                        act.copy(ends[:, h], tab[:, :, TM:NTAB])
                        for k in range(0, HOT, TM):
                            w = min(TM, HOT - k)
                            op = act.copy(slope[:, h, :, k:k + w], tab[:, :, 0:w])
                        op.then_inc(slope_ready, 1)

                    def keep_turned(m, chunks):
                        for c in chunks:
                            act.wait_ge(turned, TB * m + c + 2)
                            if exists(m - 1):
                                act.wait_ge(out_done, TB * (m - 1) + c + 2)
                            act.copy(probsT[:, c], turn_ps[:, c % 2, :].rearrange("p (b q) -> p b q", b=TB)
                                     ).then_inc(probs_ready, 1)

                    def keep_weighed(m, h):
                        act.wait_ge(out_done, TB * (m + 1) + 1)
                        if exists(m - 2):
                            act.wait_ge(y_done, m // 2 + 1)
                        act.copy(outT[:, h], out_ps[:]).then_inc(outT_ready, 1)

                    def keep_output(p):
                        act.wait_ge(y_done, p + 2)
                        act.wait_ge(y_added, p + 1)
                        act.copy(y_sb[:], small_ps[:].rearrange("p (t c) -> p t c", t=TB)).then_inc(y_kept, 1)

                    def step(pair, h, k):
                        n = pair * 2 + h
                        if h == 1 and exists(n - 4):
                            keep_output(pair - 2)
                        if exists(n - 2):
                            exponentials(n - 2, h, (k + 1) % 3)
                        if h == 1 and exists(n - 3):
                            act.wait_ge(v_done, pair + 1)
                            act.copy(v[:], small_ps[:].rearrange("p (t c) -> p t c", t=TB)).then_inc(v_ready, 1)
                        if exists(n + 1):
                            sigmoid(n + 1, 1 - h)
                        if exists(n - 3):
                            keep_turned(n - 3, (2, 3))
                        if exists(n + 1):
                            keep_table(n + 1, 1 - h)
                        if h == 0 and exists(n + 2):
                            act.wait_ge(q_done, pair + 3)
                            act.copy(qT[:], turn_ps[:, 0, :]).then_inc(qT_ready, 1)
                            act.wait_ge(k_done, pair + 3)
                            act.copy(kT[0:DH, 0], turn_ps[0:DH, 1, :])
                            act.copy(kT[DH:P, 1], turn_ps[DH:P, 1, :]).then_inc(kT_ready, 1)
                        if exists(n + 1):
                            keep_scores(n + 1, 1 - h, (k + 1) % 3)
                        if exists(n - 3):
                            keep_weighed(n - 3, 1 - h)
                        if h == 0 and exists(n - 2):
                            if exists(n - 4):
                                act.wait_ge(v_done, pair)
                            act.copy(xb[:], core.xnT[:, bass.ds((pair - 1) // d.PAIRS * S, S)]).then_inc(xb_ready, 1)
                        if exists(n - 2):
                            keep_turned(n - 2, (0, 1))

                    all_steps(act, step)

            @block.tensor
            def _(pe):
                with when(pe):
                    pe.wait_ge(table_step, 8)
                    pe.wait_ge(const_done, 12)

                    def project_qk(p):
                        pe.wait_ge(wqk_loaded, 32 * (p + 1))
                        if exists(2 * p - 5):
                            pe.wait_ge(probs_ready, TB * (2 * p - 4) + 1)
                        x = core.xnT[:, bass.ds(p // d.PAIRS * S, S)]
                        pe.matmul(turn_ps[:, 0, :], wqk[:, 0, :], x, start=True, stop=True).then_inc(q_done, 1)
                        pe.matmul(turn_ps[:, 1, :], wqk[:, 1, :], x, start=True, stop=True).then_inc(k_done, 1)

                    def project_v(p):
                        pe.wait_ge(wv_loaded, 16 * (p + 1))
                        pe.wait_ge(xb_ready, p + 2)
                        pe.wait_ge(y_kept, p + 1)
                        if exists(p * 2 + 3):
                            pe.wait_ge(slope_ready, p * 2 + 5)
                        for t in range(TB):
                            op = pe.matmul(small_ps[:, t * P:(t + 1) * P], xb[:, t * P:(t + 1) * P], wv[:],
                                           start=True, stop=True)
                        op.then_inc(v_done, 1)

                    def scores(n, p, h):
                        pe.wait_ge(kT_ready, p + 2)
                        pe.wait_ge(logits_ready, n + 1)
                        for b in range(TB):
                            op = pe.matmul(scores_ps[:, b, :], qT[:, b * P:(b + 1) * P], kT[:, h], start=True, stop=True)
                        op.then_inc(scores_done, 1)

                    def table(n, p, h):
                        for b in range(TB):
                            op = pe.matmul(small_ps[:, b * P:(b + 1) * P], qT[:, b * P:(b + 1) * P], table_w[:, h],
                                           start=True, stop=True)
                        op.then_inc(table_done, 1)

                    def turn(m, h, chunks):
                        pe.wait_ge(diag_ready, m + 2)
                        for c in chunks:
                            if c >= 2 or exists(m - 1):
                                pe.wait_ge(probs_ready, TB * m + c)
                            if c == 0 and h == 0 and exists(m + 4):
                                pe.wait_ge(kT_ready, m // 2 + 4)
                            for b in range(TB):
                                op = pe.matmul(turn_ps[:, c % 2, b * P:(b + 1) * P], chunk(h, b, c),
                                               diag[:, b, :], start=True, stop=True)
                            op.then_inc(turned, 1)

                    def weigh(m, h, chunks):
                        for c in chunks:
                            half = slice(c % 2 * DH, (c % 2 + 1) * DH)
                            pe.wait_ge(probs_ready, TB * m + c + 2)
                            if c == 0:
                                pe.wait_ge(v_ready, m // 2 + 2)
                                pe.wait_ge(outT_ready, m + 1)
                            pe.matmul(out_ps[half, :], v[:, c, h * DH:(h + 1) * DH],
                                      probsT[:, c].rearrange("p b q -> p (b q)"),
                                      start=(c < 2), stop=(c >= TB - 2)).then_inc(out_done, 1)

                    def output(p):
                        pe.wait_ge(outT_ready, 2 * (p + 1) + 1)
                        pe.wait_ge(wout_loaded, 64 * (p + 1))
                        if exists(p * 2 + 5):
                            pe.wait_ge(slope_ready, p * 2 + 7)
                        for t in range(TB):
                            for h in range(2):
                                op = pe.matmul(small_ps[:, t * P:(t + 1) * P], outT[:, h, t * P:(t + 1) * P], wout[:, h],
                                               start=(h == 0), stop=(h == 1))
                        op.then_inc(y_done, 1)

                    def step(pair, h, k):
                        n = pair * 2 + h
                        if exists(n - 3):
                            turn(n - 3, 1 - h, (2, 3))
                            if h == 1:
                                project_v(pair - 1)
                            weigh(n - 3, 1 - h, (0, 1))
                        if exists(n + 1):
                            if exists(n):
                                pe.wait_ge(slope_ready, n + 2)
                            if h == 1 and exists(n - 3):
                                pe.wait_ge(v_ready, pair + 1)
                            table(n + 1, (n + 1) // 2, 1 - h)
                        if h == 0 and exists(n + 2):
                            project_qk(pair + 1)
                        if exists(n - 3):
                            weigh(n - 3, 1 - h, (2, 3))
                        if exists(n - 2):
                            turn(n - 2, h, (0, 1))
                        if h == 0 and exists(n - 3):
                            output(pair - 2)
                        if exists(n + 2):
                            scores(n + 2, (n + 2) // 2, h)

                    all_steps(pe, step)

        nc.clear_and_free_semaphores(counted)
        nc.all_engine_barrier()


def reach_phase(nc, core, d):
    with ExitStack() as ctx:
        low = ctx.enter_context(nc.sbuf_tensor("low", [P, 1], F32))
        least = ctx.enter_context(nc.sbuf_tensor("least", [1, 1], F32))
        row_ps = ctx.enter_context(nc.psum_tensor("low_row", [1, P], F32))
        step = ctx.enter_context(nc.semaphore("reach_step"))
        with nc.Block() as block:

            @block.vector
            def _(dve):
                dve.tensor_reduce(low[:], core.reached[:], AX.X, ALU.min).then_inc(step, 1)
                dve.wait_ge(step, 2)
                dve.tensor_reduce(least[:], row_ps[:], AX.X, ALU.min).then_inc(step, 1)
                dve.wait_ge(step, 3)
                dve.tensor_scalar(core.redo[:], least[:], float(d.TMAX - 1), None, ALU.is_lt).then_inc(step, 1)
                dve.wait_ge(step, 4)

            @block.tensor
            def _(pe):
                pe.wait_ge(step, 1)
                pe.transpose(row_ps[:], low[:], core.ident[:]).then_inc(step, 1)


def residual_phase(nc, core, d, b_out):
    with ExitStack() as ctx:
        b_row = ctx.enter_context(nc.sbuf_tensor("b_row", [1, P], F32))
        bias_ps = ctx.enter_context(nc.psum_tensor("bias_ps", [P, P], F32))
        loaded = ctx.enter_context(nc.semaphore("b_loaded"))
        spread = ctx.enter_context(nc.semaphore("b_spread"))
        summed = ctx.enter_context(nc.semaphore("residual_summed"))
        with nc.Block() as block:

            @block.sync
            def _(sp):
                sp.dma_start(b_row[:], b_out).then_inc(loaded, 16)

            @block.tensor
            def _(pe):
                pe.wait_ge(loaded, 16)
                pe.matmul(bias_ps[:], core.ones_row[:], b_row[:], start=True, stop=True).then_inc(spread, 1)

            @block.vector
            def _(dve):
                dve.tensor_tensor(core.x[:], core.x[:], core.attn[:], ALU.add).then_inc(summed, 1)
                dve.wait_ge(summed, 1)
                dve.wait_ge(spread, 1)
                dve.tensor_tensor(core.x[:], core.x[:], bias_ps[:].unsqueeze(1).to_broadcast([P, d.NT, P]),
                                  ALU.add).then_inc(summed, 1)


def latent_projection_phase(nc, core, d, latT, v, Wl, bl, Wv, bo):
    S, TB = d.S, d.TB
    L = Wl.shape[1]
    with ExitStack() as ctx:
        def sb(name, shape, dt=F32):
            return ctx.enter_context(nc.sbuf_tensor("lat_" + name, shape, dt))

        counted = []

        def sem(name):
            counted.append(ctx.enter_context(nc.semaphore("lat_" + name)))
            return counted[-1]

        wl, wv = sb("wl", [P, L]), sb("wv", [P, P])
        bias, bo_row = sb("bias", [L, 1]), sb("bo_row", [1, P])
        lat = sb("lat", [P, 2, S])
        l_ps, v_ps = [ctx.enter_context(nc.psum_tensor(f"lat_{n}_ps", [P, 2, S], F32)) for n in "lv"]
        bo_ps = ctx.enter_context(nc.psum_tensor("lat_bo_ps", [P, P], F32))
        loaded, zeroed, ones_set = sem("loaded"), sem("zeroed"), sem("ones_set")
        l_done, v_done, l_out, lat_kept, v_out = sem("l_done"), sem("v_done"), sem("l_out"), sem("kept"), sem("v_out")
        bo_spread, bo_added = sem("bo_spread"), sem("bo_added")
        start_at_one(nc, counted, (loaded,))
        with nc.Block() as block:

            @block.sync
            def _(sp):
                for dst, src in ((wl[:], Wl), (bias[:], bl), (bo_row[:], bo)):
                    sp.dma_start(dst, src).then_inc(loaded, 16)
                sp.wait_ge(zeroed, 2)
                sp.dma_start(wv[0:L + 1, :], Wv).then_inc(loaded, 16)

            @block.gpsimd
            def _(pool):
                pool.memset(wv[:], 0.0).then_inc(zeroed, 1)
                pool.memset(lat[:], 0.0).then_inc(zeroed, 1)
                pool.wait_ge(zeroed, 3)
                pool.memset(lat[L:L + 1], 1.0).then_inc(ones_set, 1)
                pool.wait_ge(ones_set, 2)
                pool.memset(latT[:], 0.0).then_inc(zeroed, 1)
                pool.wait_ge(zeroed, 4)
                pool.memset(latT[L:L + 1], 1.0).then_inc(ones_set, 1)

            @block.tensor
            def _(pe):
                pe.wait_ge(loaded, 4 * 16)
                pe.wait_ge(ones_set, 2)
                pe.matmul(bo_ps[:], core.ones_row[:], bo_row[:], start=True, stop=True).then_inc(bo_spread, 1)
                with pe.Fori(0, d.B // 2) as gg:
                    for s in range(2):
                        g = gg * 2 + s
                        pe.wait_ge(l_out, g + 1)
                        pe.matmul(l_ps[0:L, s, :], wl[:], core.xnT[:, bass.ds(g * S, S)], start=True, stop=True).then_inc(l_done, 1)
                        pe.wait_ge(l_out, g + 2)
                        pe.wait_ge(v_out, g + 1)
                        for t in range(TB):
                            op = pe.matmul(v_ps[:, s, t * P:(t + 1) * P], lat[:, s, t * P:(t + 1) * P], wv[:],
                                           start=True, stop=True)
                        op.then_inc(v_done, 1)

            @block.scalar
            def _(act):
                act.wait_ge(loaded, 4 * 16)
                act.wait_ge(ones_set, 3)
                with act.Fori(0, d.B // 2) as gg:
                    for s in range(2):
                        g = gg * 2 + s
                        act.wait_ge(l_done, g + 2)
                        act.wait_ge(v_done, g + 1)
                        act.activation(lat[0:L, s, :], l_ps[0:L, s, :], ACT.Identity, bias=bias[:]).then_inc(l_out, 1)
                        act.wait_ge(l_out, g + 2)
                        act.copy(latT[0:L, bass.ds(g * S, S)], lat[0:L, s, :]).then_inc(lat_kept, 1)

            @block.vector
            def _(dve):
                dve.wait_ge(bo_spread, 2)
                dve.tensor_tensor(core.x[:], core.x[:], bo_ps[:].unsqueeze(1).to_broadcast([P, d.NT, P]),
                                  ALU.add).then_inc(bo_added, 1)
                with dve.Fori(0, d.B // 2) as gg:
                    for s in range(2):
                        g = gg * 2 + s
                        dve.wait_ge(v_done, g + 2)
                        dve.tensor_copy(v[:, bass.ds(g * S, S)], v_ps[:, s, :]).then_inc(v_out, 1)


def latent_attention_phase(nc, core, d, latT, v, Wq, bq, Wk, Wo):
    S, TB, DH, HG = d.S, d.TB, d.DH1, 4
    UNITS, GROUPS = d.B * d.HEADS1, d.HEADS1 // HG
    ITS = d.B * GROUPS
    F = HG * DH
    L3 = 3 * F
    with ExitStack() as ctx:
        def sb(name, shape, dt=F32):
            return ctx.enter_context(nc.sbuf_tensor("la_" + name, shape, dt))

        counted = []

        def sem(name):
            counted.append(nc.alloc_semaphore(name="la_" + name))
            return counted[-1]

        def ps(name, shape):
            return ctx.enter_context(nc.psum_tensor("la_" + name, shape, F32))

        wq, wk = sb("wq", [P, P]), sb("wk", [P, P])
        wo = sb("wo", [P, GROUPS, P])
        bq_cols = sb("bq_cols", [L3, GROUPS])
        wq_group, wk_group = sb("wq_group", [P, L3]), sb("wk_group", [P, L3])
        q_full = sb("q_full", [L3, S])
        q_parts = sb("q_parts", [L3, 2, S], F32R)
        k_parts = sb("k_parts", [P, 2, S], F32R)
        qh = sb("qh", [P, HG, S], F32R)
        vh = sb("vh", [P, HG, TB, 2 * F])
        own = sb("own", [P, HG])
        own_v = sb("own_v", [P, HG, F])
        own_block = sb("own_block", [TB, TB, P])
        sum_rows = sb("sum_rows", [P, P])
        row_max, neg_max = sb("row_max", [P, 2, TB]), sb("neg_max", [P, 2, TB])
        probsT = sb("probsT", [P, TB, S])
        out_sb = sb("out", [P, S])
        inverse = sb("inverse", [P, S])
        aT = sb("aT", [P, S])

        scores_ps = ps("scores_ps", [P, 2, S])
        turned_ps = ps("turned_ps", [P, 2, S])
        max_ps = ps("max_ps", [P, S])
        first_ps = ps("first_ps", [P, S])
        second_ps = ps("second_ps", [P, S])
        out_ps = ps("out_ps", [P, S])

        zeroed, loaded, set_up = sem("zeroed"), sem("loaded"), sem("set_up")
        w_ready, q_done, k_done = sem("w_ready"), sem("q_done"), sem("k_done")
        q_kept, q_hi, q_lo, k_hi, k_lo = sem("q_kept"), sem("q_hi"), sem("q_lo"), sem("k_hi"), sem("k_lo")
        qh_ready, vh_ready = sem("qh_ready"), sem("vh_ready")
        scores_done, max_done, neg_ready = sem("scores_done"), sem("max_done"), sem("neg_ready")
        max_turned, max_rows = sem("max_turned"), sem("max_rows")
        turned, exp_done, weighed = sem("turned"), sem("exp_done"), sem("weighed")
        out_kept, sum_done, inv_ready, aT_ready = sem("out_kept"), sem("sum_done"), sem("inv_ready"), sem("aT_ready")
        y_done, y_added = sem("y_done"), sem("y_added")
        wait_carried = sem("wait_carried")
        start_at_one(nc, counted, (loaded,))

        def exists(m):
            return not isinstance(m, int) or 0 <= m < UNITS

        def group(it):
            return not isinstance(it, int) or 0 <= it < ITS

        def all_steps(eng, step):
            for u in range(HG):
                step(-1, u, 1)
            for it in range(2):
                for u in range(HG):
                    step(it, u, it)
            with eng.Fori(1, ITS // 2 - 1) as pair:
                for r in range(2):
                    for u in range(HG):
                        step(pair * 2 + r, u, r)
            for it in range(ITS - 2, ITS + 1):
                for u in range(HG):
                    step(it, u, it % 2)

        with nc.Block() as block:

            @block.sync
            def _(sp):
                sp.wait_ge(zeroed, 6)
                sp.dma_start(wq[:], Wq).then_inc(loaded, 16)
                sp.dma_start(wk[0:Wk.shape[0], :], Wk).then_inc(loaded, 16)
                sp.dma_start(bq_cols[:], bq).then_inc(loaded, 16)
                for half in range(2):
                    sp.dma_start(wo[half * 2 * F:half * 2 * F + F], Wo.rearrange("(g f) c -> f g c", g=GROUPS)
                                 ).then_inc(loaded, 16)

            @block.gpsimd
            def _(pool):
                pool.memset(wk[:], 0.0).then_inc(zeroed, 1)
                pool.memset(wo[:], 0.0).then_inc(zeroed, 1)
                pool.memset(k_parts[:].bitcast(I32), 0).then_inc(zeroed, 1)
                pool.memset(qh[:].bitcast(I32), 0).then_inc(zeroed, 1)
                pool.memset(sum_rows[:], 0.0).then_inc(zeroed, 1)
                pool.memset(own[:], 1.0).then_inc(set_up, 1)
                pool.memset(own_v[:], 1.0).then_inc(set_up, 1)
                pool.memset(own_block[:], 1.0).then_inc(set_up, 1)
                pool.memset(vh[:, :, :, 0:F], 0.0).then_inc(set_up, 1)
                pool.memset(vh[:, :, :, F:2 * F], 0.0).then_inc(set_up, 1)
                pool.wait_ge(set_up, 6)
                pool.wait_ge(zeroed, 6)
                for k in range(2):
                    pool.affine_select(out=sum_rows[:], in_=sum_rows[:], compare_op=ALU.not_equal, fill=1.0,
                                       base=-(2 * k + 1) * F, pattern=[[0, P // F], [-1, F]],
                                       channel_multiplier=1).then_inc(set_up, 1)
                    pool.wait_ge(set_up, 7 + k)
                pool.affine_select(out=own_v[:], in_=own_v[:], compare_op=ALU.is_ge, fill=0.0, base=0,
                                   pattern=[[-DH, HG], [1, F]], channel_multiplier=0).then_inc(set_up, 1)
                pool.wait_ge(set_up, 9)
                pool.affine_select(out=own_v[:], in_=own_v[:], compare_op=ALU.is_ge, fill=0.0, base=DH - 1,
                                   pattern=[[DH, HG], [-1, F]], channel_multiplier=0).then_inc(set_up, 1)
                pool.wait_ge(set_up, 10)
                pool.affine_select(out=own_block[:], in_=own_block[:], compare_op=ALU.is_equal, fill=0.0, base=0,
                                   pattern=[[1, TB], [0, P]], channel_multiplier=-1).then_inc(set_up, 1)
                pool.memset(own[:], 0.0).then_inc(set_up, 1)
                for part in range(3):
                    for edge in range(DH):
                        pool.wait_ge(set_up, 12 + part * DH + edge)
                        pool.affine_select(out=own[:], in_=own[:], compare_op=ALU.not_equal, fill=1.0,
                                           base=-(part * F + edge), pattern=[[-DH, HG]],
                                           channel_multiplier=1).then_inc(set_up, 1)
                SET = 12 + 3 * DH
                pool.wait_ge(set_up, SET)
                pool.tensor_tensor(vh[:, :, :, F:2 * F], vh[:, :, :, F:2 * F],
                                   own_v[:].unsqueeze(2).to_broadcast([P, HG, TB, F]), ALU.add).then_inc(set_up, 1)
                pool.wait_ge(set_up, SET + 1)

                def low_part(it, r):
                    if exists(it * HG - 2):
                        pool.wait_ge(vh_ready, it * HG)
                    pool.wait_ge(q_hi, it + 2)
                    lo = q_parts[2 * F:L3, r, :]
                    pool.tensor_tensor(lo, q_full[2 * F:L3, :], lo, ALU.subtract).then_inc(q_lo, 1)

                def own_q(m, u, it, r):
                    pool.wait_ge(q_lo, it + 2)
                    if exists(m - HG):
                        pool.wait_ge(turned, TB * (m - HG + 1) + 1)
                    pool.sem_inc(wait_carried, 1)
                    pool.tensor_scalar(qh[0:L3, u, :], q_parts[:, r, :], own[0:L3, u:u + 1], None,
                                       ALU.mult).then_inc(qh_ready, 1)

                def own_values(m, u, it):
                    if exists(m - HG):
                        pool.wait_ge(weighed, TB * (m - HG + 1) + 1)
                    b, g = it // GROUPS, it % GROUPS
                    cols = v[:, bass.ds(b * S, S)].rearrange("p (t c) -> p t c", t=TB)[:, :, bass.ds(g * F, F)]
                    pool.sem_inc(wait_carried, 1)
                    pool.tensor_tensor(vh[:, u, :, 0:F], cols, own_v[:, u:u + 1, :].to_broadcast([P, TB, F]),
                                       ALU.mult).then_inc(vh_ready, 1)

                def normalise(it):
                    pool.wait_ge(inv_ready, TB * (it + 1) + 1)
                    if group(it - 1):
                        pool.wait_ge(y_done, it + 1)
                    pool.tensor_tensor(aT[:], out_sb[:], inverse[:], ALU.mult).then_inc(aT_ready, 1)

                def step(it, u, r):
                    n = it * HG + u
                    if u == 3 and group(it - 1):
                        normalise(it - 1)
                    if exists(n + 1):
                        own_values(n + 1, (u + 1) % HG, it if u + 1 < HG else it + 1)
                    if u == 1 and group(it + 1):
                        low_part(it + 1, 1 - r)
                    if exists(n + 3):
                        near = u + 3 < HG
                        own_q(n + 3, (u + 3) % HG, it if near else it + 1, r if near else 1 - r)

                all_steps(pool, step)

            @block.vector
            def _(dve):
                dve.wait_ge(loaded, 5 * 16)
                dve.wait_ge(zeroed, 6)
                dve.wait_ge(set_up, 13 + 3 * DH)
                dve.tensor_scalar(bq_cols[:], bq_cols[:], DH ** -0.5, None, ALU.mult).then_inc(set_up, 1)
                dve.tensor_copy(k_parts[L3:L3 + TB], core.ones_col[0:TB].unsqueeze(2).to_broadcast([TB, 2, S])
                                ).then_inc(set_up, 1)

                def group_weights(it):
                    if group(it - 1):
                        dve.wait_ge(k_done, it + 1)
                    for dst, src in ((wq_group, wq), (wk_group, wk)):
                        op = dve.tensor_copy(dst[:].rearrange("p (r f) -> p r f", f=F),
                                             src[:, bass.ds(it % GROUPS * F, F)].unsqueeze(1).to_broadcast([P, 3, F]))
                    op.then_inc(w_ready, 1)

                def max_row(m, u):
                    dve.wait_ge(max_turned, m + 2)
                    if exists(m - HG):
                        dve.wait_ge(turned, TB * (m - HG + 1) + 1)
                    dve.tensor_tensor(qh[L3:L3 + TB, u, :].rearrange("p (b q) -> p b q", b=TB),
                                      max_ps[0:TB, 0:P].unsqueeze(1).to_broadcast([TB, TB, P]), own_block[:],
                                      ALU.mult).then_inc(max_rows, 1)

                def maxima(m, u, between=None):
                    s = u % 2
                    for b in range(TB):
                        dve.wait_ge(scores_done, TB * m + b + 2)
                        dve.tensor_reduce(row_max[:, s, b:b + 1], scores_ps[:, b % 2, :], AX.X, ALU.max).then_inc(max_done, 1)
                        if between is not None:
                            between(b)
                    dve.wait_ge(max_done, TB * (m + 1) + 1)
                    dve.tensor_scalar(neg_max[:, s], row_max[:, s], -1.0, None, ALU.mult).then_inc(neg_ready, 1)

                def low_k(it, r):
                    dve.wait_ge(k_hi, it + 2)
                    lo = k_parts[F:2 * F, r, :]
                    dve.tensor_tensor(lo, second_ps[F:2 * F, :], lo, ALU.subtract).then_inc(k_lo, 1)

                def invert(it, b):
                    if b == 0:
                        dve.wait_ge(sum_done, it + 2)
                        dve.wait_ge(aT_ready, it + 1)
                    q = slice(b * P, (b + 1) * P)
                    dve.reciprocal(inverse[:, q], first_ps[:, q]).then_inc(inv_ready, 1)

                def add_output(it):
                    dve.wait_ge(y_done, it + 2)
                    dve.wait_ge(y_added, it + 1)
                    x = core.x[:, bass.ds(it // GROUPS * TB, TB), :]
                    dve.tensor_tensor(x, second_ps[:].rearrange("p (t c) -> p t c", t=TB), x, ALU.add).then_inc(y_added, 1)

                group_weights(0)

                def step(it, u, r):
                    n = it * HG + u
                    if exists(n + 1):
                        max_row(n + 1, (u + 1) % HG)
                    if u == 2 and group(it - 1):
                        between = lambda b: invert(it - 1, b)
                    else:
                        between = None
                    if exists(n + 2):
                        maxima(n + 2, (u + 2) % HG, between)
                    elif between is not None:
                        for b in range(TB):
                            between(b)
                    if u == 0 and group(it + 1):
                        low_k(it + 1, 1 - r)
                    if u == 3 and group(it - 1):
                        add_output(it - 1)
                    if u == 2 and group(it + 2):
                        group_weights(it + 2)

                all_steps(dve, step)

            @block.scalar
            def _(act):
                act.wait_ge(loaded, 5 * 16)
                act.wait_ge(set_up, 15 + 3 * DH)

                def exponentials(m, chunks):
                    for c in chunks:
                        act.wait_ge(turned, TB * m + c + 2)
                        if exists(m - 1):
                            act.wait_ge(weighed, TB * (m - 1) + c + 2)
                        act.activation(probsT[:, c, :], turned_ps[:, c % 2, :], ACT.Exp).then_inc(exp_done, 1)

                def keep_projections(it, r):
                    g = it % GROUPS
                    act.wait_ge(q_done, it + 2)
                    if group(it - 1):
                        act.wait_ge(q_lo, it + 1)
                    act.activation(q_full[:], first_ps[0:L3, :], ACT.Identity, bias=bq_cols[:, bass.ds(g, 1)],
                                   scale=DH ** -0.5).then_inc(q_kept, 1)
                    act.wait_ge(k_done, it + 2)
                    if group(it - 2):
                        act.wait_ge(turned, TB * HG * (it - 1) + 1)
                    act.copy(k_parts[0:L3, r, :], second_ps[0:L3, :]).then_inc(k_hi, 1)
                    act.wait_ge(q_kept, it + 2)
                    if group(it - 2):
                        act.wait_ge(qh_ready, HG * (it - 1) + 1)
                    act.copy(q_parts[:, r, :], q_full[:]).then_inc(q_hi, 1)

                def keep_out(it):
                    act.wait_ge(weighed, TB * HG * (it + 1) + 1)
                    act.wait_ge(sum_done, it + 1)
                    act.wait_ge(aT_ready, it + 1)
                    act.copy(out_sb[:], out_ps[:]).then_inc(out_kept, 1)

                def step(it, u, r):
                    n = it * HG + u
                    if exists(n):
                        exponentials(n, (0,))
                    if u == 0 and group(it - 1):
                        keep_out(it - 1)
                    if exists(n):
                        exponentials(n, (1, 2, 3))
                    if u == 0 and group(it + 1):
                        keep_projections(it + 1, 1 - r)

                all_steps(act, step)

            @block.tensor
            def _(pe):
                pe.wait_ge(set_up, 15 + 3 * DH)

                def project(it):
                    pe.wait_ge(w_ready, it + 2)
                    if group(it - 3):
                        pe.wait_ge(inv_ready, TB * (it - 2) + 1)
                        pe.wait_ge(y_added, it - 1)
                    b = it // GROUPS
                    pe.matmul(first_ps[0:L3, :], wq_group[:], core.xnT[:, bass.ds(b * S, S)],
                              start=True, stop=True).then_inc(q_done, 1)
                    pe.matmul(second_ps[0:L3, :], wk_group[:], latT[:, bass.ds(b * S, S)],
                              start=True, stop=True).then_inc(k_done, 1)

                def scores(m, u, it, r, b):
                    if b == 0:
                        pe.wait_ge(qh_ready, m + 2)
                        pe.wait_ge(k_lo, it + 2)
                    if b >= 2 or exists(m - 1):
                        pe.wait_ge(max_done, TB * m + b)
                    pe.matmul(scores_ps[:, b % 2, :], qh[0:L3, u, b * P:(b + 1) * P], k_parts[0:L3, r, :],
                              start=True, stop=True).then_inc(scores_done, 1)

                def turn_maxima(m, u):
                    pe.wait_ge(neg_ready, m + 2)
                    pe.wait_ge(max_rows, m + 1)
                    pe.matmul(max_ps[0:TB, 0:P], neg_max[:, u % 2, :], core.ident[:], start=True, stop=True).then_inc(max_turned, 1)

                def scores_by_keys(m, u, r, c):
                    if c == 0:
                        pe.wait_ge(max_rows, m + 2)
                    if c >= 2 or exists(m - 1):
                        pe.wait_ge(exp_done, TB * m + c)
                    pe.matmul(turned_ps[:, c % 2, :], k_parts[:, r, c * P:(c + 1) * P], qh[:, u, :],
                              start=True, stop=True).then_inc(turned, 1)

                def weigh(m, u, it, c):
                    pe.wait_ge(exp_done, TB * m + c + 2)
                    if c == 0:
                        pe.wait_ge(vh_ready, m + 2)
                        if u == 0 and group(it - 1):
                            pe.wait_ge(out_kept, it + 1)
                    half = slice(c % 2 * 2 * F, c % 2 * 2 * F + 2 * F)
                    pe.matmul(out_ps[half, :], vh[:, u, c, :], probsT[:, c, :], start=(u == 0 and c < 2),
                              stop=(u == HG - 1 and c >= 2)).then_inc(weighed, 1)

                def sums(it):
                    pe.wait_ge(out_kept, it + 2)
                    if group(it + 2):
                        pe.wait_ge(q_kept, it + 4)
                    pe.matmul(first_ps[:], sum_rows[:], out_sb[:], start=True, stop=True).then_inc(sum_done, 1)

                def output(it):
                    pe.wait_ge(aT_ready, it + 2)
                    if group(it + 2):
                        pe.wait_ge(k_lo, it + 4)
                    for t in range(TB):
                        op = pe.matmul(second_ps[:, t * P:(t + 1) * P], aT[:, t * P:(t + 1) * P],
                                       wo[:, bass.ds(it % GROUPS, 1), :].rearrange("p o c -> p (o c)"), start=True, stop=True)
                    op.then_inc(y_done, 1)

                def step(it, u, r):
                    n = it * HG + u
                    now, soon = exists(n), exists(n + 2)
                    near = u + 2 < HG
                    ahead = (n + 2, (u + 2) % HG, it if near else it + 1, r if near else 1 - r)
                    before = (n - 1, (u + HG - 1) % HG, it if u > 0 else it - 1)
                    for c in range(TB):
                        if now:
                            scores_by_keys(n, u, r, c)
                        if c < 2 and exists(n - 1):
                            weigh(*before, c + 2)
                        elif c >= 2 and now:
                            weigh(n, u, it, c - 2)
                        if soon:
                            scores(*ahead, c)
                        if c == 0 and exists(n + 1):
                            turn_maxima(n + 1, (u + 1) % HG)
                    if u == 0 and group(it + 1):
                        project(it + 1)
                    if u == 1 and group(it - 1):
                        sums(it - 1)
                    if u == 3 and group(it - 1):
                        output(it - 1)

                all_steps(pe, step)

        nc.clear_and_free_semaphores(counted)
        nc.all_engine_barrier()


def store_phase(nc, core, d, out):
    with ExitStack() as ctx:
        stored = ctx.enter_context(nc.semaphore("stored"))
        with nc.Block() as block:

            @block.sync
            def _(sp):
                view = out.rearrange("(t p) c -> p t c", p=P)
                for q in range(4):
                    k = d.NT // 4
                    sp.dma_start(view[:, q * k:(q + 1) * k, :], core.x[:, q * k:(q + 1) * k, :]).then_inc(stored, 16)
                sp.wait_ge(stored, 64)


def two_layers(nc, a, out):
    d = Dims(a["x"], a["Wq0"], a["pos_emb"], a["Wg"], a["centroidT"], a["router_wT"], a["gate_all"])
    x_in = a["x"].rearrange("b s c -> (b s) c")
    with ExitStack() as ctx:
        core = Core(nc, ctx, d)
        setup_phase(nc, core, d, x_in)

        def route0(nc, core, d, scores):
            routing_phase(nc, core, d, "_r0", scores, core.gate0[:], 2, True)

        def route1(nc, core, d, scores):
            routing_phase(nc, core, d, "_r1", scores, core.gate1[:, :, 0:d.E1], 4, False)

        norm_phase(nc, core, d, "0", route0, a["centroidT"], None)
        attention_weights = (a["Wq0"], a["Wkv"], a["Wout"], a["pos_emb"])
        cope_attention_phase(nc, core, d, "_a0", HOT, None, None, *attention_weights)
        reach_phase(nc, core, d)
        cope_attention_phase(nc, core, d, "_full", d.S, core.redo[0:1, 0:1], x_in, *attention_weights)
        hidden = [P] * (d.HC - 1) + [d.HL]
        moe_phase(nc, core, d, "_m0", a["Wg"], a["W1"], a["W2"], a["bg_cols"], a["b1_cols"], a["b2"], core.gate0, hidden)
        residual_phase(nc, core, d, a["b_out"])
        norm_phase(nc, core, d, "1", route1, a["router_wT"], a["router_bias"])
        with ExitStack() as inner:
            latT, v = (inner.enter_context(nc.sbuf_tensor("la_" + n, [P, d.T], F32)) for n in ("latT", "v"))
            latent_projection_phase(nc, core, d, latT, v, a["Wl"], a["bl"], a["Wv"], a["bo"])
            latent_attention_phase(nc, core, d, latT, v, a["Wq1"], a["bq"], a["Wk"], a["Wo"])
        moe_phase(nc, core, d, "_m1", a["gate_all"], a["up_all"], a["down_all"], None, None, None, core.gate1, [P])
        store_phase(nc, core, d, out)


HOT = 160


def lay_out(np, inp):
    f = {k: np.asarray(v) for k, v in inp.items()}
    A = np.ascontiguousarray
    E, _, H = f["L0_ffn_Wg"].shape
    D = f["L0_attn_x"].shape[-1]
    HC = -(-H // D)

    def columns(b):
        padded = np.zeros((E, HC * D), b.dtype)
        padded[:, :H] = b
        return A(padded.reshape(E, HC, D).transpose(0, 2, 1))

    def shared(w):
        return w.reshape(-1, D, D)

    gate = np.concatenate([f["L1_ffn_gate_w"], shared(f["L1_ffn_sgate_w"])])
    up = np.concatenate([f["L1_ffn_up_w"], shared(f["L1_ffn_sup_w"])])
    down = np.concatenate([f["L1_ffn_down_w"].transpose(0, 2, 1), shared(A(f["L1_ffn_sdown_w"].T))])
    return dict(
        x=A(f["L0_attn_x"][:, ::-1]), Wq0=f["L0_attn_Wq"], Wkv=f["L0_attn_Wkv"], Wout=f["L0_attn_Wout"],
        b_out=f["L0_attn_b_out"][None], pos_emb=f["L0_attn_pos_emb"], centroidT=A(f["L0_ffn_centroid"].T),
        Wg=f["L0_ffn_Wg"], W1=f["L0_ffn_W1"], W2=f["L0_ffn_W2"], bg_cols=columns(f["L0_ffn_bg"]),
        b1_cols=columns(f["L0_ffn_b1"]), b2=f["L0_ffn_b2"], Wq1=f["L1_attn_Wq"], Wl=f["L1_attn_Wl"],
        Wk=np.concatenate([f["L1_attn_Wk"], f["L1_attn_bk"][None]]),
        Wv=np.concatenate([f["L1_attn_Wv"], f["L1_attn_bv"][None]]), Wo=f["L1_attn_Wo"],
        bq=A(np.tile(f["L1_attn_bq"].reshape(4, -1).T, (3, 1))), bl=A(f["L1_attn_bl"][:, None]),
        bo=f["L1_attn_bo"][None], router_wT=A(f["L1_ffn_router_w"].T), router_bias=f["L1_ffn_router_bias"][None],
        gate_all=A(gate.transpose(0, 2, 1)), up_all=A(up.transpose(0, 2, 1)), down_all=A(down))


def kernel(**inputs):
    import numpy as _np
    import concourse.bacc as _bacc
    from concourse import mybir as _mybir
    from concourse.bass_utils import run_bass_kernel_spmd as _run

    nc = _bacc.Bacc("TRN2", target_bir_lowering=False, num_devices=1)
    arrays, args = {}, {}
    for name, a in lay_out(_np, inputs).items():
        arrays[name + "_dram"] = a
        args[name] = nc.dram_tensor(name + "_dram", a.shape, _mybir.dt.from_np(a.dtype), kind="ExternalInput").ap()
    B, S, D = inputs["L0_attn_x"].shape
    out = nc.dram_tensor("out_dram", (B * S, D), F32, kind="ExternalOutput").ap()
    two_layers(nc, args, out)
    r = _run(nc, [arrays], core_ids=[0])
    return _np.ascontiguousarray(r.results[0]["out_dram"].reshape(B, S, D)[:, ::-1])
```
